# Optimizing a Trainium2 kernel written in Bass

```python
import numpy as np
import jax
import jax.numpy as jnp

def _softmax(x, axis=-1):
    return jax.nn.softmax(x, axis=axis)

def _gelu(x):
    return jax.nn.gelu(x, approximate=True)

def _silu(x):
    return jax.nn.silu(x)

def _sigmoid(x):
    return jax.nn.sigmoid(x)

def _layernorm(x, axis=-1, eps=1e-05):
    m = jnp.mean(x, axis=axis, keepdims=True)
    v = jnp.var(x, axis=axis, keepdims=True)
    return (x - m) / jnp.sqrt(v + eps)

def _scatter_add(tgt, idx, src, axis=0):
    return tgt.at[idx].add(src)

def _segment_sum(src, seg, n):
    return jax.ops.segment_sum(src, seg, n)
kernel_name = 'mk_cond_resid_d2_seqx_r2_2d6c65'

def setup_inputs(seed: int=0):
    np.random.seed(seed)
    _w = jnp.asarray

    def _rec_inputs():
        import jax
        import jax.numpy as jnp
        _rk = jax.random.key(seed)
        x = -0.0003929 + 0.9999 * jax.random.normal(jax.random.fold_in(_rk, 1), (16, 512, 512), jnp.float32)
        _lenS = 512 - jax.random.randint(jax.random.fold_in(_rk, 7), (16,), 0, max(1, 512 // 4) + 1, jnp.int32)
        _lenS2 = 512 - jax.random.randint(jax.random.fold_in(_rk, 8), (16,), 0, max(1, 512 // 4) + 1, jnp.int32)
        cond_1024 = 0.00386106 + 1.00199 * jax.random.normal(jax.random.fold_in(_rk, 11), (16, 512), jnp.float32)
        return (x, cond_1024)
    x, cond_1024 = _rec_inputs()

    def _L0_cond_setup():
        import jax, jax.numpy as jnp
        import numpy as np
        RANK = 8
        LN_EPS = 1e-05
        key = jax.random.key(seed)
        ks = jax.random.split(key, 8)
        B, T, D = (16, 512, 512)
        A = 512
        I = 512
        OUT = D * RANK * 4
        s = 0.02
        return {'x': jax.random.normal(ks[0], (B, T, D), jnp.float32), 'ada_emb': jax.random.normal(ks[1], (B, A), jnp.float32), 'base_up': jax.random.normal(ks[2], (D, D), jnp.float32) * s, 'base_down': jax.random.normal(ks[3], (D, D), jnp.float32) * s, 'ln_gamma': jnp.ones((A,), jnp.float32), 'ln_beta': jnp.zeros((A,), jnp.float32), 'W1': jax.random.normal(ks[4], (A, I), jnp.float32) / np.sqrt(A), 'bias1': jnp.zeros((I,), jnp.float32), 'W2': jax.random.normal(ks[5], (I, OUT), jnp.float32) / np.sqrt(I), 'bias2': jnp.zeros((OUT,), jnp.float32)}
    _L0_cond_all = _L0_cond_setup()
    _L0_cond_in = {k: v for k, v in _L0_cond_all.items() if k in ('base_up', 'base_down', 'ln_gamma', 'ln_beta', 'W1', 'bias1', 'W2', 'bias2')}
    del _L0_cond_all

    def _L1_cond_setup():
        import jax, jax.numpy as jnp
        import numpy as np
        N, T, D, H = (128, 128, 512, 512)
        key = jax.random.key(seed)
        k1, k2, k3, k4 = jax.random.split(key, 4)
        x = jax.random.normal(k1, (N, T, D), dtype=jnp.float32)
        h0 = jax.random.normal(k2, (N, H), dtype=jnp.float32)
        Wx = jax.random.normal(k3, (D, H), dtype=jnp.float32) / jnp.sqrt(jnp.float32(D))
        Wh = jax.random.normal(k4, (H, H), dtype=jnp.float32) / jnp.sqrt(jnp.float32(H))
        b = jnp.zeros((H,), dtype=jnp.float32)
        return {'x': x, 'h0': h0, 'Wx': Wx, 'Wh': Wh, 'b': b}
    _L1_cond_all = _L1_cond_setup()
    _L1_cond_in = {k: v for k, v in _L1_cond_all.items() if k in ('Wx', 'Wh', 'b')}
    del _L1_cond_all
    return {'x': x, 'cond_1024': cond_1024, 'L0_cond_base_up': _L0_cond_in['base_up'], 'L0_cond_base_down': _L0_cond_in['base_down'], 'L0_cond_ln_gamma': _L0_cond_in['ln_gamma'], 'L0_cond_ln_beta': _L0_cond_in['ln_beta'], 'L0_cond_W1': _L0_cond_in['W1'], 'L0_cond_bias1': _L0_cond_in['bias1'], 'L0_cond_W2': _L0_cond_in['W2'], 'L0_cond_bias2': _L0_cond_in['bias2'], 'L1_cond_Wx': _L1_cond_in['Wx'], 'L1_cond_Wh': _L1_cond_in['Wh'], 'L1_cond_b': _L1_cond_in['b']}

def reference(x, cond_1024, L0_cond_base_up, L0_cond_base_down, L0_cond_ln_gamma, L0_cond_ln_beta, L0_cond_W1, L0_cond_bias1, L0_cond_W2, L0_cond_bias2, L1_cond_Wx, L1_cond_Wh, L1_cond_b):
    import jax
    import jax.numpy as jnp

    def _L0_cond_ref(x, ada_emb, base_up, base_down, ln_gamma, ln_beta, W1, bias1, W2, bias2):
        import jax, jax.numpy as jnp
        import numpy as np
        RANK = 8
        LN_EPS = 1e-05
        B, T, D = x.shape
        R = RANK
        mu = jnp.mean(ada_emb, axis=-1, keepdims=True)
        var = jnp.mean(jnp.square(ada_emb - mu), axis=-1, keepdims=True)
        c = (ada_emb - mu) / jnp.sqrt(var + LN_EPS) * ln_gamma + ln_beta
        h = jax.nn.gelu(c @ W1 + bias1, approximate=False)
        w = h @ W2 + bias2
        a1, b1, a2, b2 = [t.reshape(B, D, R) for t in jnp.split(w, 4, axis=-1)]
        u = jnp.einsum('btd,bdr->btr', x, a2)
        mid = jnp.einsum('btd,dl->btl', x, base_down) + jnp.einsum('btr,blr->btl', u, b2)
        mid = jax.nn.gelu(mid, approximate=False)
        v = jnp.einsum('blr,btl->btr', b1, mid)
        out = jnp.einsum('btl,kl->btk', mid, base_up) + jnp.einsum('bkr,btr->btk', a1, v)
        return x + out

    def _L1_cond_ref(x, h0, Wx, Wh, b):
        import jax, jax.numpy as jnp
        import numpy as np
        N, T, D, H = (128, 128, 512, 512)
        xW = jnp.einsum('ntd,dh->nth', x, Wx) + b

        def step(prev_h, xw_t):
            next_h = jnp.tanh(xw_t + prev_h @ Wh)
            return (next_h, next_h)
        _, hs = jax.lax.scan(step, h0, jnp.swapaxes(xW, 0, 1))
        return jnp.swapaxes(hs, 0, 1)
    x = x + _L0_cond_ref(x, cond_1024, L0_cond_base_up, L0_cond_base_down, L0_cond_ln_gamma, L0_cond_ln_beta, L0_cond_W1, L0_cond_bias1, L0_cond_W2, L0_cond_bias2)
    x = x + _L1_cond_ref(x, cond_1024, L1_cond_Wx, L1_cond_Wh, L1_cond_b)
    return x

_drawn_inputs = setup_inputs


def setup_inputs(seed=0):
    import zlib

    import numpy as np

    out = dict(_drawn_inputs(seed))
    spreads = {'L0_cond_ln_gamma': (1.0, 0.2),
     'L0_cond_ln_beta': (0.0, 0.1),
     'L0_cond_bias1': (0.0, 0.1),
     'L0_cond_bias2': (0.0, 0.1),
     'L1_cond_b': (0.0, 0.8)}
    factors = {'L0_cond_base_up': 3.8, 'L0_cond_base_down': 3.737, 'L1_cond_Wx': 8.0, 'L1_cond_Wh': 8.0}
    for name, (base, spread) in spreads.items():
        noise = np.random.default_rng([zlib.crc32(name.encode()), seed]).standard_normal(out[name].shape)
        drawn = base * np.exp(spread * noise) if base else spread * noise
        out[name] = jnp.asarray(drawn.astype(out[name].dtype))
    for name, factor in factors.items():
        out[name] = (out[name] * factor).astype(out[name].dtype)
    return out
```

```python
from contextlib import ExitStack

import concourse.bass as bass
from concourse import mybir

P = 128
F32 = mybir.dt.float32
F32R = mybir.dt.float32r
BF16 = mybir.dt.bfloat16
U32 = mybir.dt.uint32
ALU = mybir.AluOpType
ACT = mybir.ActivationFunctionType
AX = mybir.AxisListType

RANK = 8
LN_EPS = 1e-5
PARTS = 3
GROUPS = 2
REPS = 2
HI, LO = 0, 1
PASSES = ((HI, HI), (HI, LO), (LO, HI))
BULK_BANKS = 6

BANK_Y = (2, 3, 4, 5)
BANK_XT = (0, 1, 2, 3)
BANK_U = 4
BANK_MID = (5, 0, 1, 2)
BANK_V = 3
BANK_OUT = (4, 5, 0, 1)
BANK_XW = (4, 5, 0, 1)

SLOT_Y = 0
SLOT_XT = (1, 2)
SLOT_U = (3, 6)
SLOT_MID = (6, 14)
SLOT_V = (14, 16)
SLOT_OUT = (16, 24)
SLOT_XW = (24, 32)


def build(nc: bass.Bass, x, cond, down, up, gamma, beta, w1, bias1, w2, bias2, wx, wh, b, y):
    B, T, D = x.shape
    KT = D // P
    TC = 512 // B
    NC = T // TC
    COLS = B * TC
    JB = P // TC
    JT = B // JB
    GB = B // GROUPS
    GC = GB * TC
    QUARTER = D * RANK
    W2C = P * RANK
    assert COLS == 512 and GB * RANK * REPS == P and NC % 2 == 0 and KT == JT == 4 and TC == 32

    with ExitStack() as ctx:
        def sb(name, shape, dt=F32):
            return ctx.enter_context(nc.sbuf_tensor(name, shape, dt))

        def psum(name, shape, dt=F32):
            return ctx.enter_context(nc.psum_tensor(name, shape, dt))

        def sem(name):
            return ctx.enter_context(nc.semaphore(name))

        down_s = sb("down_s", [P, 2, KT, D], F32R)
        up_s = sb("up_s", [P, 2, KT, D], F32R)
        wx_s = sb("wx_s", [P, 2, KT, D], F32R)
        wh_s = sb("wh_s", [P, PARTS, KT, D], BF16)
        a2_s = sb("a2_s", [P, 2, KT, GROUPS, P], F32R)
        b1_s = sb("b1_s", [P, 2, KT, GROUPS, P], F32R)
        b2_s = sb("b2_s", [P, 2, GROUPS, D], F32R)
        a1_s = sb("a1_s", [P, 2, GROUPS, D], F32R)

        work = sb("work", [P, 3, 4096])
        x1 = work[:, 0, :].rearrange("p (s k n) -> p s k n", s=2, k=KT)
        xw = work[:, 1, :].rearrange("p (s k n) -> p s k n", s=2, k=KT)
        xn = work[:, 2, 0:2048].rearrange("p (j n) -> p j n", j=JT)
        yn = work[:, 2, 2048:4096].rearrange("p (j n) -> p j n", j=JT)
        stage = sb("stage", [P, 2, KT, D])
        act_s = sb("act_s", [P, 2, KT, COLS], F32R)
        mid_s = sb("mid_s", [P, 2, KT, COLS], F32R)
        gel = sb("gel", [P, 2, COLS])
        rank = sb("rank", [P, COLS])
        rank_hi = sb("rank_hi", [P, COLS], F32R)
        rank_s = sb("rank_s", [P, COLS], F32R)
        mask = sb("mask", [P, COLS], U32)
        mask_b = sb("mask_b", [P, 2, GB])
        mask_i = sb("mask_i", [P, GB], U32)
        negsel = sb("negsel", [P, 1])
        ident = sb("ident", [P, P])
        z = sb("z", [P, 2, KT, B])
        hf = sb("hf", [P, 4, KT, B])
        hs = sb("hs", [P, KT, PARTS, B], BF16)
        seen = sb("seen", [P, 1])
        hrem = sb("hrem", [P, KT, B])
        cn = work[0:B, 2, 2048:2048 + 2 * D].rearrange("b (s d) -> b s d", s=2)
        ln = sb("ln", [B, 8])
        cT = sb("cT", [P, KT, B])
        hT = sb("hT", [P, KT, B])
        vecs = work[0:4 * KT, 2, 3072:3072 + P]
        vT = sb("vT", [P, 4, KT])
        bias2T = sb("bias2T", [P, 4, KT, RANK])
        fac = sb("fac", [P, 2, GROUPS, REPS, GB, RANK])

        rec = psum("rec", [P, 2, 512])
        R = [rec[:, i, 0:KT * 4 * B].rearrange("p (m j b) -> p m j b", m=KT, j=4) for i in range(2)]
        bulk = psum("bulk", [P, BULK_BANKS, 512])

        cond_in = sem("cond_in")
        vec_in = sem("vec_in")
        vec_tr = sem("vec_tr")
        vT_done = sem("vT_done")
        small_in = sem("small_in")
        w1_in = sem("w1_in")
        stage_in = [sem(f"stage_in{i}") for i in range(2)]
        w2_in = [sem(f"w2_in{i}") for i in range(3)]
        x_in = [sem(f"x_in{j}") for j in range(JT)]
        y_out = [sem(f"y_out{j}") for j in range(JT)]
        pool_set = sem("pool_set")
        chain = sem("chain")
        sqrt_done = sem("sqrt_done")
        cond_tr = sem("cond_tr")
        cT_done = sem("cT_done")
        hT_mm = sem("hT_mm")
        hT_done = sem("hT_done")
        up_tr = sem("up_tr")
        stage_used = sem("stage_used")
        wsplit = sem("wsplit")
        fac_mm = sem("fac_mm")
        fac_done = sem("fac_done")
        fac_tr = sem("fac_tr")
        fac_split = sem("fac_split")
        h0_done = sem("h0_done")
        y_tr = sem("y_tr")
        x_tr = sem("x_tr")
        u_mm = sem("u_mm")
        mid_mm = sem("mid_mm")
        v_mm = sem("v_mm")
        out_mm = sem("out_mm")
        xw_mm = sem("xw_mm")
        rec_mm = sem("rec_mm")
        y_act = sem("y_act")
        y_dve = sem("y_dve")
        x2_done = sem("x2_done")
        xlo_done = sem("xlo_done")
        rank_sel = sem("rank_sel")
        rank_rnd = sem("rank_rnd")
        rank_done = sem("rank_done")
        gel_done = sem("gel_done")
        mhi_done = sem("mhi_done")
        mid_done = sem("mid_done")
        x1_done = sem("x1_done")
        x1hi_done = sem("x1hi_done")
        x1lo_done = sem("x1lo_done")
        xw_done = sem("xw_done")
        z_done = sem("z_done")
        tanh_done = sem("tanh_done")
        rem_done = sem("rem_done")
        h_done = sem("h_done")
        xw_placed = sem("xw_placed")
        sum_done = sem("sum_done")

        w2_v = w2.rearrange("(k p) n -> p k n", p=P)
        W2_TILES = [(q, dt) for q in (2, 3, 1, 0) for dt in range(KT)]

        def need(eng, s, n):
            if not isinstance(n, int) or n > 0:
                eng.wait_ge(s, n)

        def dma_x(eng, c, j):
            for i in range(JB):
                eng.dma_start(xn[i * TC:(i + 1) * TC, j, :],
                              x[j * JB + i, bass.ds(c * TC, TC), :]).then_inc(x_in[j], 16)

        block = ctx.enter_context(nc.Block())

        def run_chunks(eng, chunk):
            chunk(-1, 0, recur=False, y_on=False)
            chunk(0, 0, y_on=False)
            with eng.Fori(0, (NC - 2) // 2) as i:
                chunk(i * 2 + 1, 1)
                chunk(i * 2 + 2, 0)
            chunk(NC - 1, 1, bulk_on=False)
            chunk(NC, 0, recur=False, bulk_on=False)

        @block.sync
        def _(sp):
            sp.dma_start(cn[:, 0, :], cond).then_inc(cond_in, 16)
            for v, vec in enumerate((gamma, beta, bias1, b)):
                sp.dma_start(vecs[v * KT:(v + 1) * KT, :], vec.rearrange("(k p) -> k p", p=P)).then_inc(vec_in, 16)
            for q in range(4):
                sp.dma_start(bias2T[:, q], bias2[q * QUARTER:(q + 1) * QUARTER].rearrange(
                    "(k p r) -> p k r", p=P, r=RANK)).then_inc(small_in, 16)
            sp.dma_start(work[:, 2, 0:2048].rearrange("p (k n) -> p k n", k=KT),
                         w1.rearrange("(k p) n -> p k n", p=P)).then_inc(w1_in, 16)

            def load_w2(n):
                q, dt = W2_TILES[n]
                if n == 2:
                    sp.wait_ge(hT_mm, 1)
                if n >= 3:
                    sp.wait_ge(fac_mm, n - 2)
                c0 = q * QUARTER + dt * W2C
                sp.dma_start(work[:, n % 3, :].rearrange("p (k n) -> p k n", k=KT),
                             w2_v[:, :, c0:c0 + W2C]).then_inc(w2_in[n % 3], 16)

            load_w2(0)
            load_w2(1)
            for n, w in enumerate((down, up)):
                sp.dma_start(stage[:, n], w.rearrange("(k p) n -> p k n", p=P)).then_inc(stage_in[n], 16)
            load_w2(2)
            load_w2(3)
            for n, w in enumerate((wx, wh)):
                if n == 0:
                    sp.wait_ge(stage_used, 1)
                else:
                    sp.wait_ge(up_tr, KT)
                sp.dma_start(stage[:, n], w.rearrange("(k p) n -> p k n", p=P)).then_inc(stage_in[n], 16)
            for n in range(4, len(W2_TILES)):
                load_w2(n)
            sp.wait_ge(fac_mm, len(W2_TILES))
            for j in range(JT):
                dma_x(sp, 0, j)
            with sp.Fori(1, NC) as c:
                sp.wait_ge(x_tr, c * KT)
                for j in range(JT):
                    dma_x(sp, c, j)
            for j in range(JT):
                sp.wait_ge(y_out[j], 16 * JB * NC)

        @block.gpsimd
        def _(pool):
            nc.gpsimd.memset(ident[:], 0.0).then_inc(pool_set, 1)
            nc.gpsimd.memset(mask_b[:], 1.0).then_inc(pool_set, 1)
            pool.wait_ge(pool_set, 2)
            nc.gpsimd.affine_select(out=ident[:], in_=ident[:], compare_op=ALU.not_equal, fill=1.0, base=0,
                                    pattern=[[-1, P]], channel_multiplier=1).then_inc(pool_set, 1)
            for rep in range(REPS):
                m = mask_b[:, rep, :]
                base = -rep * GB * RANK
                nc.gpsimd.affine_select(out=m, in_=m, compare_op=ALU.is_ge, fill=0.0, base=base,
                                        pattern=[[-RANK, GB]], channel_multiplier=1).then_inc(pool_set, 1)
                pool.wait_ge(pool_set, 4 + 2 * rep)
                nc.gpsimd.affine_select(out=m, in_=m, compare_op=ALU.is_ge, fill=0.0, base=RANK - 1 - base,
                                        pattern=[[RANK, GB]], channel_multiplier=-1).then_inc(pool_set, 1)

            def chunk(c, par, recur=True, bulk_on=True, y_on=True):
                if not recur:
                    return
                for t in range(TC):
                    n = c * TC + t
                    if t == 0:
                        need(pool, x1lo_done, (c + 1) * KT)
                    pool.wait_ge(tanh_done, n + 1)
                    xs = x1[:, par].rearrange("p k (b t) -> p k b t", t=TC)[:, :, :, t]
                    nc.gpsimd.tensor_tensor(xs, xs, hf[:, t % 4], ALU.add).then_inc(sum_done, 1)

            run_chunks(pool, chunk)

        @block.scalar
        def _(act):
            act.wait_ge(chain, 5)
            nc.scalar.activation(ln[:, 4:5], ln[:, 3:4], ACT.Sqrt).then_inc(sqrt_done, 1)
            act.wait_ge(hT_mm, 1)
            act.wait_ge(vT_done, 1)
            for m in range(KT):
                last = nc.scalar.activation(hT[:, m, :], bulk[:, 1, m * B:(m + 1) * B], ACT.Gelu,
                                            bias=vT[:, 2, m:m + 1])
            last.then_inc(hT_done, 1)

            def place(c, par, t):
                nc.scalar.activation(R[t % 2][:, :, 3, :],
                                     xw[:, par].rearrange("p k (b t) -> p k b t", t=TC)[:, :, :, t],
                                     ACT.Copy).then_inc(xw_placed, 1)

            def store_y(c, j):
                for i in range(JB):
                    act.dma_start(y[j * JB + i, bass.ds(c * TC, TC), :],
                                  yn[i * TC:(i + 1) * TC, j, :]).then_inc(y_out[j], 16)

            def chunk(c, par, recur=True, bulk_on=True, y_on=True):
                nxt, np_ = c + 1, 1 - par if recur else par
                for t in range(TC):
                    if recur:
                        n = c * TC + t
                        act.wait_ge(z_done, n + 1)
                        nc.scalar.activation(hs[:, :, 0, :], z[:, t % 2], ACT.Tanh)
                        if not (isinstance(n, int) and n < 4):
                            act.wait_ge(sum_done, n - 3)
                        nc.scalar.activation(hf[:, t % 4], z[:, t % 2], ACT.Tanh).then_inc(tanh_done, 1)
                        if t + 2 < TC:
                            place(c, par, t + 2)
                    if y_on and t == SLOT_Y:
                        for j in (0, 1):
                            act.wait_ge(y_tr, (c - 1) * JT + j + 1)
                            nc.scalar.copy(yn[:, j, :], bulk[:, BANK_Y[j], :]).then_inc(y_act, 1)
                        for j in (0, 1):
                            act.wait_ge(y_act, (c - 1) * 2 + j + 1)
                            store_y(c - 1, j)
                        for j in (2, 3):
                            act.wait_ge(y_dve, (c - 1) * 2 + j - 1)
                            store_y(c - 1, j)
                    if y_on and t == TC - 1:
                        for j in (0, 1):
                            act.wait_ge(y_out[j], 16 * JB * c)
                    if not bulk_on:
                        continue
                    if t in SLOT_XT:
                        for k in (2 * (t - SLOT_XT[0]), 2 * (t - SLOT_XT[0]) + 1):
                            act.wait_ge(x_tr, nxt * KT + k + 1)
                            if k == 0:
                                need(act, xw_mm, nxt * KT)
                            nc.scalar.copy(act_s[:, HI, k], bulk[:, BANK_XT[k], :])
                            if k == 0 and y_on:
                                act.wait_ge(y_tr, c * JT)
                            nc.scalar.mul(x1[:, np_, k], bulk[:, BANK_XT[k], :], 2.0).then_inc(x2_done, 1)
                    if SLOT_MID[0] <= t < SLOT_MID[1] and (t - SLOT_MID[0]) % 2:
                        m = (t - SLOT_MID[0]) // 2
                        act.wait_ge(mid_mm, nxt * KT + m + 1)
                        need(act, mid_done, nxt * KT + m - 1)
                        nc.scalar.activation(gel[:, m % 2], bulk[:, BANK_MID[m], :], ACT.Gelu).then_inc(gel_done, 1)
                    if SLOT_OUT[0] <= t < SLOT_OUT[1] and (t - SLOT_OUT[0]) % 2:
                        m = (t - SLOT_OUT[0]) // 2
                        act.wait_ge(x1_done, nxt * KT + m + 1)
                        nc.scalar.copy(act_s[:, HI, m], x1[:, np_, m]).then_inc(x1hi_done, 1)
                    if SLOT_XW[0] <= t < SLOT_XW[1] and (t - SLOT_XW[0]) % 2:
                        m = (t - SLOT_XW[0]) // 2
                        act.wait_ge(xw_mm, nxt * KT + m + 1)
                        nc.scalar.activation(xw[:, np_, m], bulk[:, BANK_XW[m], :], ACT.Identity,
                                             bias=vT[:, 3, m:m + 1]).then_inc(xw_done, 1)
                if bulk_on:
                    if recur:
                        act.wait_ge(z_done, (c + 1) * TC)
                    act.wait_ge(xw_done, nxt * KT + KT)
                    place(nxt, np_, 0)
                    place(nxt, np_, 1)

            run_chunks(act, chunk)

        @block.vector
        def _(dve):
            links = [0]

            def link(ins):
                links[0] += 1
                ins.then_inc(chain, 1)
                dve.wait_ge(chain, links[0])

            dve.wait_ge(cond_in, 16)
            link(nc.vector.tensor_reduce(ln[:, 0:1], cn[:, 0, :], AX.X, ALU.add))
            link(nc.vector.tensor_scalar(ln[:, 1:2], ln[:, 0:1], 1.0 / D, None, ALU.mult))
            link(nc.vector.tensor_scalar(cn[:, 1, :], cn[:, 0, :], ln[:, 1:2], None, ALU.subtract))
            link(nc.vector.tensor_tensor_reduce(out=gel[0:B, 0, :], in0=cn[:, 1, :], in1=cn[:, 1, :], scale=1.0,
                                                scalar=0.0, op0=ALU.mult, op1=ALU.add, accum_out=ln[:, 2:3]))
            link(nc.vector.tensor_scalar(ln[:, 3:4], ln[:, 2:3], 1.0 / D, LN_EPS, ALU.mult, ALU.add))
            dve.wait_ge(sqrt_done, 1)
            link(nc.vector.reciprocal(ln[:, 5:6], ln[:, 4:5]))
            link(nc.vector.tensor_scalar(ln[:, 6:7], ln[:, 5:6], ln[:, 5:6], ln[:, 3:4], ALU.mult, ALU.mult))
            link(nc.vector.tensor_scalar(ln[:, 7:8], ln[:, 6:7], -0.5, 1.5, ALU.mult, ALU.add))
            link(nc.vector.tensor_scalar(ln[:, 6:7], ln[:, 7:8], ln[:, 5:6], None, ALU.mult))
            link(nc.vector.tensor_scalar(cn[:, 1, :], cn[:, 1, :], ln[:, 6:7], None, ALU.mult))
            dve.wait_ge(vec_tr, 1)
            nc.vector.tensor_copy(vT[:], bulk[:, 2, 0:4 * KT].rearrange("p (v k) -> p v k", v=4)).then_inc(vT_done, 1)
            dve.wait_ge(cond_tr, 1)
            dve.wait_ge(vT_done, 1)
            dve.wait_ge(small_in, 64)
            for k in range(KT):
                last = nc.vector.tensor_scalar(cT[:, k, :], bulk[:, 0, k * B:(k + 1) * B], vT[:, 0, k:k + 1],
                                               vT[:, 1, k:k + 1], ALU.mult, ALU.add)
            last.then_inc(cT_done, 1)
            h0 = bulk[:, 0, KT * B:2 * KT * B].rearrange("p (k b) -> p k b", k=KT)
            link(nc.vector.tensor_copy(hs[:, :, 0, :], h0))
            link(nc.vector.tensor_tensor(hrem[:], h0, hs[:, :, 0, :], ALU.subtract))
            link(nc.vector.tensor_copy(hs[:, :, 1, :], hrem[:]))
            nc.vector.tensor_tensor(hs[:, :, 2, :], hrem[:], hs[:, :, 1, :], ALU.subtract).then_inc(h0_done, 1)

            nc.vector.memset(negsel[0:P // 2, :], 0.0)
            nc.vector.memset(negsel[P // 2:P, :], -1.0)
            nc.vector.memset(rank[:], 0.0)
            dve.wait_ge(pool_set, 7)
            link(nc.vector.tensor_tensor(mask_i[:], mask_b[:, 0, :], mask_b[:, 1, :], ALU.add))
            mv = mask[:].rearrange("p (g b t) -> p g b t", g=GROUPS, t=TC)
            for g in range(GROUPS):
                last = nc.vector.tensor_copy(mv[:, g], mask_i[:].rearrange("p (b o) -> p b o", o=1)
                                             .broadcast_to([P, GB, TC]))
            link(last)

            def split(dst, n):
                link(nc.vector.tensor_copy(dst[:, HI], stage[:, n]))
                nc.vector.tensor_tensor(dst[:, LO], stage[:, n], dst[:, HI].bitcast(F32),
                                        ALU.subtract).then_inc(stage_used, 1)

            def factor(n):
                q, dt = W2_TILES[n]
                f = fac[:, n % 2]
                dve.wait_ge(fac_mm, n + 1)
                if n >= 2:
                    dve.wait_ge(fac_split, n - 1)
                pw = bulk[:, 2 + n % 2, 0:RANK * B].rearrange("p (r g b) -> p g b r", r=RANK, g=GROUPS)
                bias = bias2T[:, q, dt:dt + 1, :].broadcast_to([P, GB, RANK])
                for rep in range(REPS):
                    for g in range(GROUPS):
                        last = nc.vector.tensor_tensor(f[:, g, rep], pw[:, g], bias, ALU.add)
                last.then_inc(fac_done, 1)
                if q in (1, 2):
                    dst = (b1_s if q == 1 else a2_s)[:, :, dt].rearrange("p s g n -> p s (g n)")
                    src = f.rearrange("p g e b r -> p (g e b r)")
                    dve.wait_ge(fac_done, n + 1)
                else:
                    dst = (a1_s if q == 0 else b2_s)[:, :, :, dt * P:(dt + 1) * P]
                    src = bulk[:, 4 + n % 2, 0:GROUPS * P].rearrange("p (g n) -> p g n", g=GROUPS)
                    dve.wait_ge(fac_tr, (n % 8) - 3 if n < 8 else (n - 12) + 5)
                link(nc.vector.tensor_copy(dst[:, HI], src))
                nc.vector.tensor_tensor(dst[:, LO], src, dst[:, HI].bitcast(F32), ALU.subtract).then_inc(fac_split, 1)

            dve.wait_ge(stage_in[0], 16)
            split(down_s, 0)
            for k in range(KT):
                dve.wait_ge(up_tr, k + 1)
                src = bulk[:, 4 + k % 2, :]
                link(nc.vector.tensor_copy(up_s[:, HI, k], src))
                nc.vector.tensor_tensor(up_s[:, LO, k], src, up_s[:, HI, k].bitcast(F32),
                                        ALU.subtract).then_inc(wsplit, 1)
            for n in range(4):
                factor(n)
            dve.wait_ge(stage_in[0], 32)
            split(wx_s, 0)
            for n in range(4, 6):
                factor(n)
            dve.wait_ge(stage_in[1], 32)
            link(nc.vector.tensor_copy(wh_s[:, 0], stage[:, 1]))
            link(nc.vector.tensor_tensor(stage[:, 1], stage[:, 1], wh_s[:, 0], ALU.subtract))
            for n in range(6, 8):
                factor(n)
            link(nc.vector.tensor_copy(wh_s[:, 1], stage[:, 1]))
            link(nc.vector.tensor_tensor(wh_s[:, 2], stage[:, 1], wh_s[:, 1], ALU.subtract))
            for n in range(8, len(W2_TILES)):
                factor(n)

            def chunk(c, par, recur=True, bulk_on=True, y_on=True):
                nxt, np_ = c + 1, 1 - par if recur else par
                for t in range(TC):
                    if recur:
                        n = c * TC + t
                        dve.wait_ge(rec_mm, n + 1)
                        nc.vector.tensor_reduce(z[:, t % 2], R[t % 2].rearrange("p m j b -> p m b j"), AX.X,
                                                ALU.add).then_inc(z_done, 1)
                        dve.wait_ge(tanh_done, n + 1)
                        nc.vector.tensor_tensor(hrem[:], hf[:, t % 4], hs[:, :, 0, :], ALU.subtract)
                        nc.vector.tensor_tensor(hs[:, :, 1, :], hf[:, t % 4], hs[:, :, 0, :],
                                                ALU.subtract).then_inc(rem_done, 1)
                        dve.wait_ge(rem_done, n + 1)
                        nc.vector.tensor_tensor(hs[:, :, 2, :], hrem[:], hs[:, :, 1, :],
                                                ALU.subtract).then_inc(h_done, 1)
                    if y_on and t == SLOT_Y:
                        for j in (2, 3):
                            dve.wait_ge(y_tr, (c - 1) * JT + j + 1)
                            nc.vector.tensor_copy(yn[:, j, :], bulk[:, BANK_Y[j], :]).then_inc(y_dve, 1)
                    if y_on and t == TC - 1:
                        for j in (2, 3):
                            dve.wait_ge(y_out[j], 16 * JB * c)
                    if not bulk_on:
                        continue
                    if t in SLOT_XT:
                        for k in (2 * (t - SLOT_XT[0]), 2 * (t - SLOT_XT[0]) + 1):
                            dve.wait_ge(x2_done, nxt * KT + k + 1)
                            nc.vector.scalar_tensor_tensor(out=act_s[:, LO, k], in0=x1[:, np_, k], scalar=0.5,
                                                           in1=act_s[:, HI, k].bitcast(F32), op0=ALU.mult,
                                                           op1=ALU.subtract).then_inc(xlo_done, 1)
                    if t == SLOT_U[1] - 1 or t == SLOT_V[1] - 1:
                        s, bank, e = (u_mm, BANK_U, 0) if t == SLOT_U[1] - 1 else (v_mm, BANK_V, 1)
                        dve.wait_ge(s, nxt + 1)
                        nc.vector.tensor_copy(seen[:], bulk[:, bank, 0:1])
                        nc.vector.copy_predicated(rank[:], mask[:], bulk[:, bank, :]).then_inc(rank_sel, 1)
                        dve.wait_ge(rank_sel, 2 * nxt + e + 1)
                        nc.vector.tensor_copy(rank_hi[:], rank[:]).then_inc(rank_rnd, 1)
                        dve.wait_ge(rank_rnd, 2 * nxt + e + 1)
                        if e == 0:
                            need(dve, out_mm, nxt * KT)
                        else:
                            dve.wait_ge(mid_mm, (nxt + 1) * KT)
                        nc.vector.scalar_tensor_tensor(out=rank_s[:], in0=rank_hi[:].bitcast(F32),
                                                       scalar=negsel[:, 0:1], in1=rank[:], op0=ALU.mult,
                                                       op1=ALU.add).then_inc(rank_done, 1)
                    if SLOT_MID[0] < t - 1 < SLOT_MID[1] and (t - 1 - SLOT_MID[0]) % 2:
                        m = (t - 1 - SLOT_MID[0]) // 2
                        dve.wait_ge(gel_done, nxt * KT + m + 1)
                        if m == 0:
                            need(dve, out_mm, nxt * KT)
                        nc.vector.tensor_copy(mid_s[:, HI, m], gel[:, m % 2]).then_inc(mhi_done, 1)
                        dve.wait_ge(mhi_done, nxt * KT + m + 1)
                        nc.vector.tensor_tensor(mid_s[:, LO, m], gel[:, m % 2], mid_s[:, HI, m].bitcast(F32),
                                                ALU.subtract).then_inc(mid_done, 1)
                    if SLOT_OUT[0] < t < SLOT_OUT[1] and (t - SLOT_OUT[0]) % 2:
                        m = (t - SLOT_OUT[0]) // 2
                        dve.wait_ge(out_mm, nxt * KT + m + 1)
                        dve.wait_ge(x2_done, nxt * KT + m + 1)
                        nc.vector.tensor_tensor(x1[:, np_, m], bulk[:, BANK_OUT[m], :], x1[:, np_, m],
                                                ALU.add).then_inc(x1_done, 1)
                    if SLOT_OUT[0] < t - 1 < SLOT_OUT[1] and (t - 1 - SLOT_OUT[0]) % 2:
                        m = (t - 1 - SLOT_OUT[0]) // 2
                        dve.wait_ge(x1hi_done, nxt * KT + m + 1)
                        nc.vector.tensor_tensor(act_s[:, LO, m], x1[:, np_, m], act_s[:, HI, m].bitcast(F32),
                                                ALU.subtract).then_inc(x1lo_done, 1)

            run_chunks(dve, chunk)

        @block.tensor
        def _(pe):
            pe.wait_ge(pool_set, 3)
            pe.wait_ge(vec_in, 64)
            nc.tensor.transpose(bulk[:, 2, 0:4 * KT], vecs, ident[0:4 * KT, 0:4 * KT]).then_inc(vec_tr, 1)
            pe.wait_ge(chain, 10)
            for k in range(KT):
                nc.tensor.transpose(bulk[:, 0, k * B:(k + 1) * B], cn[:, 1, k * P:(k + 1) * P], ident[0:B, 0:B])
            for k in range(KT):
                last = nc.tensor.transpose(bulk[:, 0, (KT + k) * B:(KT + k + 1) * B], cn[:, 0, k * P:(k + 1) * P],
                                           ident[0:B, 0:B])
            last.then_inc(cond_tr, 1)
            pe.wait_ge(cT_done, 1)
            pe.wait_ge(w1_in, 16)
            w1_v = work[:, 2, 0:2048].rearrange("p (k n) -> p k n", k=KT)
            for m in range(KT):
                for k in range(KT):
                    last = nc.tensor.matmul(bulk[:, 1, m * B:(m + 1) * B], w1_v[:, k, m * P:(m + 1) * P], cT[:, k, :],
                                            start=(k == 0), stop=(k == KT - 1))
            last.then_inc(hT_mm, 1)
            pe.wait_ge(stage_in[1], 16)
            for k in range(KT):
                if k >= 2:
                    pe.wait_ge(wsplit, k - 1)
                for n in range(KT):
                    last = nc.tensor.transpose(bulk[:, 4 + k % 2, n * P:(n + 1) * P],
                                               stage[:, 1, n, k * P:(k + 1) * P], ident[:])
                last.then_inc(up_tr, 1)
            pe.wait_ge(wsplit, KT)
            pe.wait_ge(hT_done, 1)

            def turn(n):
                pe.wait_ge(fac_done, n + 1)
                if n >= 2:
                    pe.wait_ge(fac_split, n - 1)
                for g in range(GROUPS):
                    last = nc.tensor.transpose(bulk[:, 4 + n % 2, g * P:(g + 1) * P],
                                               fac[:, n % 2, g].rearrange("p e b r -> p (e b r)"), ident[:])
                last.then_inc(fac_tr, 1)

            for n, (q, dt) in enumerate(W2_TILES):
                pe.wait_ge(w2_in[n % 3], 16 * (n // 3 + 1))
                if n >= 2:
                    pe.wait_ge(fac_done, n - 1)
                wv = work[:, n % 3, :].rearrange("p (k d r) -> p k d r", k=KT, r=RANK)
                for r in range(RANK):
                    for k in range(KT):
                        last = nc.tensor.matmul(bulk[:, 2 + n % 2, r * B:(r + 1) * B], wv[:, k, :, r], hT[:, k, :],
                                                start=(k == 0), stop=(k == KT - 1))
                last.then_inc(fac_mm, 1)
                if n >= 1 and W2_TILES[n - 1][0] in (0, 3):
                    turn(n - 1)
            turn(len(W2_TILES) - 1)
            pe.wait_ge(fac_split, len(W2_TILES))
            pe.wait_ge(h0_done, 1)

            def rank_in(out_bank, fac_s, src, lo, hi):
                for i in range(lo, hi):
                    k, g, p = i // 6, i // 3 % 2, i % 3
                    a, w = PASSES[p]
                    last = nc.tensor.matmul(bulk[:, out_bank, g * GC:(g + 1) * GC], fac_s[:, w, k, g, :],
                                            src[:, a, k, g * GC:(g + 1) * GC], start=(i == 0), stop=(i >= 20),
                                            skip_group_check=True)
                return last

            def dense(banks, w_s, src, rank_f, i):
                per = len(PASSES) * KT + (2 * GROUPS if rank_f is not None else 0)
                m, r = i // per, i % per
                if r < len(PASSES) * KT:
                    k, (a, w) = r // 3, PASSES[r % 3]
                    return nc.tensor.matmul(bulk[:, banks[m], :], w_s[:, w, k, m * P:(m + 1) * P], src[:, a, k, :],
                                            start=(r == 0), stop=(r == per - 1), skip_group_check=True)
                w, g = (r - 12) % 2, (r - 12) // 2
                return nc.tensor.matmul(bulk[:, banks[m], g * GC:(g + 1) * GC], rank_f[:, w, g, m * P:(m + 1) * P],
                                        rank_s[:, g * GC:(g + 1) * GC], start=False, stop=(r == per - 1),
                                        skip_group_check=True)

            def chunk(c, par, recur=True, bulk_on=True, y_on=True):
                nxt, np_ = c + 1, 1 - par if recur else par
                for t in range(TC):
                    if recur:
                        n = c * TC + t
                        pe.wait_ge(xw_placed, n + 1)
                        need(pe, h_done, n)
                        for m in range(KT):
                            for k in range(KT):
                                for q in range(PARTS):
                                    last = nc.tensor.matmul(R[t % 2][:, m, 0:PARTS, :],
                                                            wh_s[:, q, k, m * P:(m + 1) * P], hs[:, k, :, :],
                                                            start=(k == 0 and q == 0),
                                                            stop=(k == KT - 1 and q == PARTS - 1),
                                                            skip_group_check=True)
                        last.then_inc(rec_mm, 1)
                    if y_on and t == SLOT_Y:
                        pe.wait_ge(sum_done, c * TC)
                        for j in range(JT):
                            if j >= 2 and recur:
                                pe.wait_ge(xw_done, c * KT + j - 1)
                            for k in range(KT):
                                last = nc.tensor.transpose(bulk[:, BANK_Y[j], k * P:(k + 1) * P],
                                                           x1[:, 1 - par, k, j * P:(j + 1) * P], ident[:])
                            last.then_inc(y_tr, 1)
                    if not bulk_on:
                        continue
                    if t in SLOT_XT:
                        for k in (2 * (t - SLOT_XT[0]), 2 * (t - SLOT_XT[0]) + 1):
                            if k < 2:
                                need(pe, xw_done, nxt * KT)
                            elif y_on:
                                pe.wait_ge(y_act, (c - 1) * 2 + k - 1)
                            for j in range(JT):
                                if k == 0:
                                    pe.wait_ge(x_in[j], 16 * JB * (nxt + 1))
                                last = nc.tensor.transpose(bulk[:, BANK_XT[k], j * P:(j + 1) * P],
                                                           xn[:, j, k * P:(k + 1) * P], ident[:])
                            last.then_inc(x_tr, 1)
                    if SLOT_U[0] <= t < SLOT_U[1]:
                        lo, hi = 8 * (t - SLOT_U[0]), 8 * (t - SLOT_U[0]) + 8
                        if t == SLOT_U[0] and y_on:
                            pe.wait_ge(y_dve, (c - 1) * 2 + 2)
                        for k in range(KT):
                            if lo <= 6 * k < hi or (k == 3 and t == SLOT_U[1] - 1):
                                pe.wait_ge(xlo_done, nxt * KT + k + 1)
                        last = rank_in(BANK_U, a2_s, act_s, lo, hi)
                        if t == SLOT_U[1] - 1:
                            last.then_inc(u_mm, 1)
                    if SLOT_MID[0] <= t < SLOT_MID[1]:
                        for i in range(8 * (t - SLOT_MID[0]), 8 * (t - SLOT_MID[0]) + 8):
                            if i % 16 == 0 and i:
                                pe.wait_ge(x2_done, nxt * KT + i // 16)
                            if i == 12:
                                pe.wait_ge(rank_done, 2 * nxt + 1)
                            last = dense(BANK_MID, down_s, act_s, b2_s, i)
                            if i % 16 == 15:
                                last.then_inc(mid_mm, 1)
                    if SLOT_V[0] <= t < SLOT_V[1]:
                        lo, hi = 12 * (t - SLOT_V[0]), 12 * (t - SLOT_V[0]) + 12
                        if lo == 0:
                            pe.wait_ge(x2_done, (nxt + 1) * KT)
                        for k in (lo // 6, lo // 6 + 1):
                            pe.wait_ge(mid_done, nxt * KT + k + 1)
                            last = rank_in(BANK_V, b1_s, mid_s, 6 * k, 6 * k + 6)
                        if hi == 24:
                            last.then_inc(v_mm, 1)
                    if SLOT_OUT[0] <= t < SLOT_OUT[1]:
                        for i in range(8 * (t - SLOT_OUT[0]), 8 * (t - SLOT_OUT[0]) + 8):
                            if i == 0:
                                pe.wait_ge(rank_sel, 2 * nxt + 1)
                            if i % 16 == 0 and i:
                                pe.wait_ge(gel_done, nxt * KT + i // 16)
                            if i == 12:
                                pe.wait_ge(rank_done, 2 * nxt + 2)
                            last = dense(BANK_OUT, up_s, mid_s, a1_s, i)
                            if i % 16 == 15:
                                last.then_inc(out_mm, 1)
                    if SLOT_XW[0] <= t < SLOT_XW[1]:
                        for i in range(6 * (t - SLOT_XW[0]), 6 * (t - SLOT_XW[0]) + 6):
                            if i < 12 and i % 3 == 0:
                                pe.wait_ge(x1lo_done, nxt * KT + i // 3 + 1)
                            last = dense(BANK_XW, wx_s, act_s, None, i)
                            if i % 12 == 11:
                                last.then_inc(xw_mm, 1)

            run_chunks(pe, chunk)


_INS = ["x", "cond_1024", "L0_cond_base_down", "L0_cond_base_up", "L0_cond_ln_gamma", "L0_cond_ln_beta", "L0_cond_W1",
        "L0_cond_bias1", "L0_cond_W2", "L0_cond_bias2", "L1_cond_Wx", "L1_cond_Wh", "L1_cond_b"]


def kernel(**inputs):
    import numpy as _np
    import concourse.bacc as _bacc
    from concourse import mybir as _mybir
    from concourse.bass_utils import run_bass_kernel_spmd as _run

    nc = _bacc.Bacc("TRN2", target_bir_lowering=False, num_devices=1)
    arrays, args = {}, []
    for name in _INS:
        a = _np.ascontiguousarray(inputs[name])
        arrays[f"in_{name}_dram"] = a
        args.append(nc.dram_tensor(f"in_{name}_dram", a.shape, _mybir.dt.from_np(a.dtype), kind="ExternalInput").ap())
    out = nc.dram_tensor("out_0_dram", inputs["x"].shape, _mybir.dt.float32, kind="ExternalOutput").ap()
    build(nc, *args, out)
    r = _run(nc, [arrays], core_ids=[0])
    return r.results[0]["out_0_dram"]
```

```python
from contextlib import ExitStack

import concourse.bass as bass
from concourse import mybir

P = 128
F32 = mybir.dt.float32
F32R = mybir.dt.float32r
BF16 = mybir.dt.bfloat16
U32 = mybir.dt.uint32
ALU = mybir.AluOpType
ACT = mybir.ActivationFunctionType
AX = mybir.AxisListType

RANK = 8
LN_EPS = 1e-5
PARTS = 3
GROUPS = 2
REPS = 2
HI, LO = 0, 1
PASSES = ((HI, HI), (HI, LO), (LO, HI))
BULK_BANKS = 6

BANK_XT = (0, 1, 3, 0)
BANK_Y = (2, 4, 1, 2)
BANK_U = 5
BANK_MID = (3, 4, 0, 1)
BANK_V = 2
BANK_OUT = (5, 3, 4, 0)
BANK_XW = (1, 2, 5, 3)


def portions(costs, slots):
    total, out, i, at = sum(costs), [], 0, 0.0
    for n in range(slots):
        first = i
        while i < len(costs) and at + costs[i] / 2 <= total * (n + 1) / slots:
            at += costs[i]
            i += 1
        out.append((first, i if n < slots - 1 else len(costs)))
    return out


def dense_items(kt, rank):
    main = [[(m, k, p) for k in range(kt) for p in range(len(PASSES))] for m in range(kt)]
    low = [[(m, g, -1 - w) for g in range(GROUPS) for w in (HI, LO)] for m in range(kt)]
    if rank:
        items = main[0] + main[1][:6] + low[0] + main[1][6:] + low[1]
    else:
        items = main[0][:9] + main[1][:9] + main[0][9:] + main[1][9:]
    for m in range(2, kt):
        items += main[m] + (low[m] if rank else [])
    return items


SLOT_XT = (0, 4)
SLOT_Y = (1, 5)
SLOT_U = (2, 6)
SLOT_MID = (6, 14)
SLOT_V = (14, 16)
SLOT_OUT = (16, 24)
SLOT_XW = (24, 32)


def build(nc: bass.Bass, x, cond, down, up, gamma, beta, w1, bias1, w2, bias2, wx, wh, b, y):
    B, T, D = x.shape
    KT = D // P
    TC = 512 // B
    NC = T // TC
    HT = KT // 2
    COLS = B * TC
    JB = P // TC
    JT = B // JB
    GB = B // GROUPS
    GC = GB * TC
    QUARTER = D * RANK
    W2C = P * RANK
    assert COLS == 512 and GB * RANK * REPS == P and NC % 2 == 0 and KT == JT == 4 and TC == 32

    with ExitStack() as ctx:
        def sb(name, shape, dt=F32):
            return ctx.enter_context(nc.sbuf_tensor(name, shape, dt))

        def psum(name, shape, dt=F32):
            return ctx.enter_context(nc.psum_tensor(name, shape, dt))

        def sem(name):
            return ctx.enter_context(nc.semaphore(name))

        down_s = sb("down_s", [P, 2, KT, D], F32R)
        up_s = sb("up_s", [P, 2, KT, D], F32R)
        wx_s = sb("wx_s", [P, 2, KT, D], F32R)
        wh_s = sb("wh_s", [P, PARTS, KT, D], BF16)
        a2_s = sb("a2_s", [P, 2, KT, GROUPS, P], F32R)
        b1_s = sb("b1_s", [P, 2, KT, GROUPS, P], F32R)
        b2_s = sb("b2_s", [P, 2, GROUPS, D], F32R)
        a1_s = sb("a1_s", [P, 2, GROUPS, D], F32R)

        RING = 5
        work = sb("work", [P, RING + 1, KT * 512])
        x1 = work[:, 0:2, :].rearrange("p s (k n) -> p s k n", k=KT)
        xw = work[:, 2:4, :].rearrange("p s (k n) -> p s k n", k=KT)
        xn = work[:, 4, :].rearrange("p (j n) -> p j n", j=JT)
        yn = work[:, 5, :].rearrange("p (j n) -> p j n", j=JT)
        stage = sb("stage", [P, 2, KT, D])
        act_s = sb("act_s", [P, 2, KT, COLS], F32R)
        mid_s = sb("mid_s", [P, 2, KT, COLS], F32R)
        gel = sb("gel", [P, 2, COLS])
        rank = sb("rank", [P, COLS])
        rank_hi = sb("rank_hi", [P, COLS], F32R)
        rank_s = sb("rank_s", [P, COLS], F32R)
        mask = sb("mask", [P, COLS], U32)
        mask_b = sb("mask_b", [P, 2, GB])
        mask_i = sb("mask_i", [P, GB], U32)
        negsel = sb("negsel", [P, 1])
        ident = sb("ident", [P, P])
        z = sb("z", [P, KT, B])
        hf = sb("hf", [P, 4, KT, B])
        hs = sb("hs", [P, KT, PARTS, B], BF16)
        seen = sb("seen", [P, 1])
        hrem = sb("hrem", [P, KT, B])
        wrow = work[0:B, 5, :].rearrange("b (s n) -> b s n", s=2)
        cn = work[0:B, 5, 0:2 * D].rearrange("b (s d) -> b s d", s=2)
        vecs = work[0:4 * KT, 5, 2 * D:2 * D + P]
        ln = sb("ln", [B, 8])
        cT = sb("cT", [P, KT, B])
        hT = sb("hT", [P, KT, B])
        vT = sb("vT", [P, 4, KT])
        bias2T = sb("bias2T", [P, 4, KT, RANK])
        fac = sb("fac", [P, 2, GROUPS, REPS, GB, RANK])

        rec = psum("rec", [P, 2, 512])
        R = [rec[:, f, 0:HT * 4 * B].rearrange("p (m j b) -> p m j b", m=HT, j=4) for f in range(2)]
        bulk = psum("bulk", [P, BULK_BANKS, 512])

        cond_in = sem("cond_in")
        vec_in = sem("vec_in")
        vec_tr = sem("vec_tr")
        vT_done = sem("vT_done")
        small_in = sem("small_in")
        w1_in = sem("w1_in")
        stage_in = [sem(f"stage_in{i}") for i in range(2)]
        w2_in = [sem(f"w2_in{i}") for i in range(RING)]
        x_in = [sem(f"x_in{j}") for j in range(JT)]
        y_out = [sem(f"y_out{j}") for j in range(JT)]
        pool_set = sem("pool_set")
        chain = sem("chain")
        sqrt_done = sem("sqrt_done")
        cond_tr = sem("cond_tr")
        cT_done = sem("cT_done")
        hT_mm = sem("hT_mm")
        hT_done = sem("hT_done")
        up_tr = sem("up_tr")
        stage_used = sem("stage_used")
        wsplit = sem("wsplit")
        row_mm = sem("row_mm")
        row_done = sem("row_done")
        fac_mm = sem("fac_mm")
        fac_done = sem("fac_done")
        fac_tr = sem("fac_tr")
        fac_split = sem("fac_split")
        h0_done = sem("h0_done")
        y_tr = sem("y_tr")
        x_tr = sem("x_tr")
        u_mm = sem("u_mm")
        mid_mm = sem("mid_mm")
        v_mm = sem("v_mm")
        out_mm = sem("out_mm")
        xw_mm = sem("xw_mm")
        rec_mm = sem("rec_mm")
        y_done = sem("y_done")
        xhi_done = sem("xhi_done")
        xlo_done = sem("xlo_done")
        rank_sel = sem("rank_sel")
        rank_rnd = sem("rank_rnd")
        rank_done = sem("rank_done")
        gel_done = sem("gel_done")
        mid_done = sem("mid_done")
        x1_part = sem("x1_part")
        x1_done = sem("x1_done")
        x1hi_done = sem("x1hi_done")
        x1lo_done = sem("x1lo_done")
        xw_done = sem("xw_done")
        z_done = sem("z_done")
        tanh_done = sem("tanh_done")
        rem_done = sem("rem_done")
        h_done = sem("h_done")
        xw_placed = sem("xw_placed")
        sum_done = sem("sum_done")

        w2_v = w2.rearrange("(k p) n -> p k n", p=P)
        W2_TILES = [(q, dt) for q in (2, 3, 1, 0) for dt in range(KT)]

        def need(eng, s, n):
            if not isinstance(n, int) or n > 0:
                eng.wait_ge(s, n)

        def dma_x(eng, c, j):
            for i in range(JB):
                eng.dma_start(xn[i * TC:(i + 1) * TC, j, :],
                              x[j * JB + i, bass.ds(c * TC, TC), :]).then_inc(x_in[j], 16)

        block = ctx.enter_context(nc.Block())

        def plan(rank, slots):
            items = dense_items(KT, rank)
            parts = portions([1 if p >= 0 else 0.5 for _, _, p in items], slots[1] - slots[0])
            ends = {max(i for i, it in enumerate(items) if it[0] == m): m for m in range(KT)}
            starts = {min(i for i, it in enumerate(items) if it[0] == m): m for m in range(KT)}
            at = {m: slots[0] + next(n for n, (a, z) in enumerate(parts) if a <= i < z) for i, m in ends.items()}
            return items, parts, starts, ends, at

        MID, OUT, XW = plan(True, SLOT_MID), plan(True, SLOT_OUT), plan(False, SLOT_XW)
        MID_AT, OUT_AT, XW_AT = MID[-1], OUT[-1], XW[-1]

        def tile_at(at, t):
            return [m for m in range(KT) if at[m] == t]

        def run_chunks(eng, chunk):
            chunk(-1, 0, recur=False, y_on=False)
            chunk(0, 0, y_on=False)
            with eng.Fori(0, (NC - 2) // 2) as i:
                chunk(i * 2 + 1, 1)
                chunk(i * 2 + 2, 0)
            chunk(NC - 1, 1, bulk_on=False)
            chunk(NC, 0, recur=False, bulk_on=False)

        @block.sync
        def _(sp):
            sp.dma_start(cn[:, 0, :], cond).then_inc(cond_in, 16)
            for v, vec in enumerate((gamma, beta, bias1, b)):
                sp.dma_start(vecs[v * KT:(v + 1) * KT, :], vec.rearrange("(k p) -> k p", p=P)).then_inc(vec_in, 16)
            for q in range(4):
                sp.dma_start(bias2T[:, q], bias2[q * QUARTER:(q + 1) * QUARTER].rearrange(
                    "(k p r) -> p k r", p=P, r=RANK)).then_inc(small_in, 16)
            sp.dma_start(work[:, RING - 1, :].rearrange("p (k n) -> p k n", k=KT),
                         w1.rearrange("(k p) n -> p k n", p=P)).then_inc(w1_in, 16)

            def load_w2(n):
                q, dt = W2_TILES[n // 2]
                if n == RING - 1:
                    sp.wait_ge(hT_mm, 1)
                if n >= RING:
                    sp.wait_ge(row_mm, n - RING + 1)
                c0 = q * QUARTER + dt * W2C + n % 2 * 512
                sp.dma_start(work[:, n % RING, :].rearrange("p (k n) -> p k n", k=KT),
                             w2_v[:, :, c0:c0 + 512]).then_inc(w2_in[n % RING], 16)

            for n in range(RING - 1):
                load_w2(n)
            for n, w in enumerate((down, up)):
                sp.dma_start(stage[:, n], w.rearrange("(k p) n -> p k n", p=P)).then_inc(stage_in[n], 16)
            for n in range(RING - 1, 2 * RING):
                load_w2(n)
            for n, w in enumerate((wx, wh)):
                if n == 0:
                    sp.wait_ge(stage_used, 1)
                else:
                    sp.wait_ge(up_tr, KT)
                sp.dma_start(stage[:, n], w.rearrange("(k p) n -> p k n", p=P)).then_inc(stage_in[n], 16)
            for n in range(2 * RING, 2 * len(W2_TILES)):
                load_w2(n)
            sp.wait_ge(row_mm, 2 * len(W2_TILES) - 2)
            for j in range(JT):
                dma_x(sp, 0, j)

            def next_x(c):
                sp.wait_ge(x_tr, c * KT)
                for j in range(JT):
                    dma_x(sp, c, j)

            def store_y(c):
                for j in range(JT):
                    sp.wait_ge(y_done, c * JT + j + 1)
                    for i in range(JB):
                        sp.dma_start(y[j * JB + i, bass.ds(c * TC, TC), :],
                                     yn[i * TC:(i + 1) * TC, j, :]).then_inc(y_out[j], 16)

            next_x(1)
            next_x(2)
            with sp.Fori(0, NC - 3) as c:
                next_x(c + 3)
                store_y(c)
            for c in range(NC - 3, NC):
                store_y(c)
            for j in range(JT):
                sp.wait_ge(y_out[j], 16 * JB * NC)

        @block.gpsimd
        def _(pool):
            nc.gpsimd.memset(ident[:], 0.0).then_inc(pool_set, 1)
            nc.gpsimd.memset(mask_b[:], 1.0).then_inc(pool_set, 1)
            pool.wait_ge(pool_set, 2)
            nc.gpsimd.affine_select(out=ident[:], in_=ident[:], compare_op=ALU.not_equal, fill=1.0, base=0,
                                    pattern=[[-1, P]], channel_multiplier=1).then_inc(pool_set, 1)
            for rep in range(REPS):
                m = mask_b[:, rep, :]
                base = -rep * GB * RANK
                nc.gpsimd.affine_select(out=m, in_=m, compare_op=ALU.is_ge, fill=0.0, base=base,
                                        pattern=[[-RANK, GB]], channel_multiplier=1).then_inc(pool_set, 1)
                pool.wait_ge(pool_set, 4 + 2 * rep)
                nc.gpsimd.affine_select(out=m, in_=m, compare_op=ALU.is_ge, fill=0.0, base=RANK - 1 - base,
                                        pattern=[[RANK, GB]], channel_multiplier=-1).then_inc(pool_set, 1)

            def chunk(c, par, recur=True, bulk_on=True, y_on=True):
                if not recur:
                    return
                for t in range(TC):
                    n = c * TC + t
                    if t == 0:
                        need(pool, x1lo_done, (c + 1) * KT)
                    pool.wait_ge(tanh_done, 2 * n + 2)
                    xs = x1[:, par].rearrange("p k (b t) -> p k b t", t=TC)[:, :, :, t]
                    nc.gpsimd.tensor_tensor(xs, xs, hf[:, t % 4], ALU.add).then_inc(sum_done, 1)

            run_chunks(pool, chunk)

        @block.scalar
        def _(act):
            act.wait_ge(chain, 5)
            nc.scalar.activation(ln[:, 4:5], ln[:, 3:4], ACT.Sqrt).then_inc(sqrt_done, 1)
            act.wait_ge(hT_mm, 1)
            act.wait_ge(vT_done, 1)
            for m in range(KT):
                last = nc.scalar.activation(hT[:, m, :], bulk[:, 1, m * B:(m + 1) * B], ACT.Gelu,
                                            bias=vT[:, 2, m:m + 1])
            last.then_inc(hT_done, 1)

            for n in range(2 * len(W2_TILES)):
                act.wait_ge(row_mm, n + 1)
                if n >= 4:
                    act.wait_ge(fac_mm, n // 2 - 1)
                nc.scalar.copy(wrow[:, n // 2 % 2, n % 2 * 512:n % 2 * 512 + 512],
                               bulk[0:B, 2 + n % 2, :]).then_inc(row_done, 1)

            def place(par, t, f):
                nc.scalar.activation(R[f][:, :, 3, :],
                                     xw[:, par].rearrange("p k (b t) -> p k b t", t=TC)[:, f * HT:(f + 1) * HT, :, t],
                                     ACT.Copy).then_inc(xw_placed, 1)

            def chunk(c, par, recur=True, bulk_on=True, y_on=True):
                nxt, np_ = c + 1, 1 - par if recur else par
                for t in range(TC):
                    for f in range(2) if recur else ():
                        n = c * TC + t
                        half = slice(f * HT, (f + 1) * HT)
                        act.wait_ge(z_done, 2 * n + f + 1)
                        nc.scalar.activation(hs[:, half, 0, :], z[:, half], ACT.Tanh)
                        if f == 0 and not (isinstance(n, int) and n < 4):
                            act.wait_ge(sum_done, n - 3)
                        nc.scalar.activation(hf[:, t % 4, half], z[:, half], ACT.Tanh).then_inc(tanh_done, 1)
                        if t + 1 < TC:
                            place(par, t + 1, f)
                    if bulk_on and SLOT_XT[0] <= t < SLOT_XT[1]:
                        k = t - SLOT_XT[0]
                        act.wait_ge(x_tr, nxt * KT + k + 1)
                        if k == 0:
                            need(act, xw_mm, nxt * KT)
                        nc.scalar.copy(act_s[:, HI, k], bulk[:, BANK_XT[k], :]).then_inc(xhi_done, 1)
                    if y_on and SLOT_Y[0] <= t < SLOT_Y[1]:
                        j = t - SLOT_Y[0]
                        act.wait_ge(y_tr, (c - 1) * JT + j + 1)
                        nc.scalar.copy(yn[:, j, :], bulk[:, BANK_Y[j], :]).then_inc(y_done, 1)
                    if y_on and recur and t == TC - 1:
                        for j in range(JT):
                            act.wait_ge(y_out[j], 16 * JB * c)
                    if not bulk_on:
                        continue
                    for m in tile_at(MID_AT, t):
                        act.wait_ge(mid_mm, nxt * KT + m + 1)
                        need(act, mid_done, nxt * KT + m - 1)
                        if m == 0:
                            need(act, out_mm, nxt * KT)
                        nc.scalar.activation(gel[:, m % 2], bulk[:, BANK_MID[m], :], ACT.Gelu)
                        nc.scalar.activation(mid_s[:, HI, m], bulk[:, BANK_MID[m], :],
                                             ACT.Gelu).then_inc(gel_done, 1)
                    for m in tile_at(OUT_AT, t - 1):
                        act.wait_ge(x1_done, nxt * KT + m + 1)
                        nc.scalar.copy(act_s[:, HI, m], x1[:, np_, m]).then_inc(x1hi_done, 1)
                    for m in tile_at(XW_AT, t):
                        act.wait_ge(xw_mm, nxt * KT + m + 1)
                        nc.scalar.activation(xw[:, np_, m], bulk[:, BANK_XW[m], :], ACT.Identity,
                                             bias=vT[:, 3, m:m + 1]).then_inc(xw_done, 1)
                if bulk_on:
                    for f in range(2):
                        if recur:
                            act.wait_ge(z_done, 2 * TC * (c + 1) - 1 + f)
                        act.wait_ge(xw_done, nxt * KT + (f + 1) * HT)
                        place(np_, 0, f)

            run_chunks(act, chunk)

        @block.vector
        def _(dve):
            links = [0]

            def link(ins):
                links[0] += 1
                ins.then_inc(chain, 1)
                dve.wait_ge(chain, links[0])

            dve.wait_ge(cond_in, 16)
            link(nc.vector.tensor_reduce(ln[:, 0:1], cn[:, 0, :], AX.X, ALU.add))
            link(nc.vector.tensor_scalar(ln[:, 1:2], ln[:, 0:1], 1.0 / D, None, ALU.mult))
            link(nc.vector.tensor_scalar(cn[:, 1, :], cn[:, 0, :], ln[:, 1:2], None, ALU.subtract))
            link(nc.vector.tensor_tensor_reduce(out=gel[0:B, 0, :], in0=cn[:, 1, :], in1=cn[:, 1, :], scale=1.0,
                                                scalar=0.0, op0=ALU.mult, op1=ALU.add, accum_out=ln[:, 2:3]))
            link(nc.vector.tensor_scalar(ln[:, 3:4], ln[:, 2:3], 1.0 / D, LN_EPS, ALU.mult, ALU.add))
            dve.wait_ge(sqrt_done, 1)
            link(nc.vector.reciprocal(ln[:, 5:6], ln[:, 4:5]))
            link(nc.vector.tensor_scalar(ln[:, 6:7], ln[:, 5:6], ln[:, 5:6], ln[:, 3:4], ALU.mult, ALU.mult))
            link(nc.vector.tensor_scalar(ln[:, 7:8], ln[:, 6:7], -0.5, 1.5, ALU.mult, ALU.add))
            link(nc.vector.tensor_scalar(ln[:, 6:7], ln[:, 7:8], ln[:, 5:6], None, ALU.mult))
            link(nc.vector.tensor_scalar(cn[:, 1, :], cn[:, 1, :], ln[:, 6:7], None, ALU.mult))
            dve.wait_ge(vec_tr, 1)
            nc.vector.tensor_copy(vT[:], bulk[:, 2, 0:4 * KT].rearrange("p (v k) -> p v k", v=4)).then_inc(vT_done, 1)
            dve.wait_ge(cond_tr, 1)
            dve.wait_ge(vT_done, 1)
            dve.wait_ge(small_in, 64)
            for k in range(KT):
                last = nc.vector.tensor_scalar(cT[:, k, :], bulk[:, 0, k * B:(k + 1) * B], vT[:, 0, k:k + 1],
                                               vT[:, 1, k:k + 1], ALU.mult, ALU.add)
            last.then_inc(cT_done, 1)
            h0 = bulk[:, 0, KT * B:2 * KT * B].rearrange("p (k b) -> p k b", k=KT)
            link(nc.vector.tensor_copy(hs[:, :, 0, :], h0))
            link(nc.vector.tensor_tensor(hrem[:], h0, hs[:, :, 0, :], ALU.subtract))
            link(nc.vector.tensor_copy(hs[:, :, 1, :], hrem[:]))
            nc.vector.tensor_tensor(hs[:, :, 2, :], hrem[:], hs[:, :, 1, :], ALU.subtract).then_inc(h0_done, 1)

            nc.vector.memset(negsel[0:P // 2, :], 0.0)
            nc.vector.memset(negsel[P // 2:P, :], -1.0)
            nc.vector.memset(rank[:], 0.0)
            dve.wait_ge(pool_set, 7)
            link(nc.vector.tensor_tensor(mask_i[:], mask_b[:, 0, :], mask_b[:, 1, :], ALU.add))
            mv = mask[:].rearrange("p (g b t) -> p g b t", g=GROUPS, t=TC)
            for g in range(GROUPS):
                last = nc.vector.tensor_copy(mv[:, g], mask_i[:].rearrange("p (b o) -> p b o", o=1)
                                             .broadcast_to([P, GB, TC]))
            link(last)

            def split(dst, n):
                link(nc.vector.tensor_copy(dst[:, HI], stage[:, n]))
                nc.vector.tensor_tensor(dst[:, LO], stage[:, n], dst[:, HI].bitcast(F32),
                                        ALU.subtract).then_inc(stage_used, 1)

            def factor(n):
                q, dt = W2_TILES[n]
                f = fac[:, n % 2]
                dve.wait_ge(fac_mm, n + 1)
                if n >= 2:
                    dve.wait_ge(fac_split, n - 1)
                pw = bulk[:, n % 2, 0:RANK * B].rearrange("p (r g b) -> p g b r", r=RANK, g=GROUPS)
                bias = bias2T[:, q, dt:dt + 1, :].broadcast_to([P, GB, RANK])
                for rep in range(REPS):
                    for g in range(GROUPS):
                        last = nc.vector.tensor_tensor(f[:, g, rep], pw[:, g], bias, ALU.add)
                last.then_inc(fac_done, 1)
                if q in (1, 2):
                    dst = (b1_s if q == 1 else a2_s)[:, :, dt].rearrange("p s g n -> p s (g n)")
                    src = f.rearrange("p g e b r -> p (g e b r)")
                    dve.wait_ge(fac_done, n + 1)
                else:
                    dst = (a1_s if q == 0 else b2_s)[:, :, :, dt * P:(dt + 1) * P]
                    src = bulk[:, 4 + n % 2, 0:GROUPS * P].rearrange("p (g n) -> p g n", g=GROUPS)
                    dve.wait_ge(fac_tr, (n % 8) - 3 if n < 8 else (n - 12) + 5)
                link(nc.vector.tensor_copy(dst[:, HI], src))
                nc.vector.tensor_tensor(dst[:, LO], src, dst[:, HI].bitcast(F32), ALU.subtract).then_inc(fac_split, 1)

            dve.wait_ge(stage_in[0], 16)
            split(down_s, 0)
            for k in range(KT):
                dve.wait_ge(up_tr, k + 1)
                src = bulk[:, 4 + k % 2, :]
                link(nc.vector.tensor_copy(up_s[:, HI, k], src))
                nc.vector.tensor_tensor(up_s[:, LO, k], src, up_s[:, HI, k].bitcast(F32),
                                        ALU.subtract).then_inc(wsplit, 1)
            for n in range(4):
                factor(n)
            dve.wait_ge(stage_in[0], 32)
            split(wx_s, 0)
            for n in range(4, 6):
                factor(n)
            dve.wait_ge(stage_in[1], 32)
            link(nc.vector.tensor_copy(wh_s[:, 0], stage[:, 1]))
            link(nc.vector.tensor_tensor(stage[:, 1], stage[:, 1], wh_s[:, 0], ALU.subtract))
            for n in range(6, 8):
                factor(n)
            link(nc.vector.tensor_copy(wh_s[:, 1], stage[:, 1]))
            link(nc.vector.tensor_tensor(wh_s[:, 2], stage[:, 1], wh_s[:, 1], ALU.subtract))
            for n in range(8, len(W2_TILES)):
                factor(n)

            def chunk(c, par, recur=True, bulk_on=True, y_on=True):
                nxt, np_ = c + 1, 1 - par if recur else par
                for t in range(TC):
                    if recur:
                        n = c * TC + t
                        for f in range(2):
                            dve.wait_ge(rec_mm, 2 * n + f + 1)
                            nc.vector.tensor_reduce(z[:, f * HT:(f + 1) * HT], R[f].rearrange("p m j b -> p m b j"),
                                                    AX.X, ALU.add).then_inc(z_done, 1)
                        for f in range(2):
                            half = slice(f * HT, (f + 1) * HT)
                            dve.wait_ge(tanh_done, 2 * n + f + 1)
                            nc.vector.tensor_tensor(hs[:, half, 1, :], hf[:, t % 4, half], hs[:, half, 0, :],
                                                    ALU.subtract)
                            nc.vector.tensor_tensor(hrem[:, half], hf[:, t % 4, half], hs[:, half, 0, :],
                                                    ALU.subtract).then_inc(rem_done, 1)
                            dve.wait_ge(rem_done, 2 * n + f + 1)
                            nc.vector.tensor_tensor(hs[:, half, 2, :], hrem[:, half], hs[:, half, 1, :],
                                                    ALU.subtract).then_inc(h_done, 1)
                    if not bulk_on:
                        continue
                    if SLOT_XT[0] <= t < SLOT_XT[1]:
                        k = t - SLOT_XT[0]
                        dve.wait_ge(xhi_done, nxt * KT + k + 1)
                        nc.vector.tensor_tensor(act_s[:, LO, k], bulk[:, BANK_XT[k], :],
                                                act_s[:, HI, k].bitcast(F32), ALU.subtract).then_inc(xlo_done, 1)
                    for e, last_slot, mm, bank in ((0, SLOT_U[1] - 1, u_mm, BANK_U), (1, SLOT_V[1] - 1, v_mm, BANK_V)):
                        if t == last_slot:
                            dve.wait_ge(mm, nxt + 1)
                            nc.vector.tensor_copy(seen[:], bulk[:, bank, 0:1])
                            nc.vector.copy_predicated(rank[:], mask[:], bulk[:, bank, :]).then_inc(rank_sel, 1)
                        if t == last_slot + 1:
                            dve.wait_ge(rank_sel, 2 * nxt + e + 1)
                            nc.vector.tensor_copy(rank_hi[:], rank[:]).then_inc(rank_rnd, 1)
                            dve.wait_ge(rank_rnd, 2 * nxt + e + 1)
                            if e == 0:
                                need(dve, out_mm, nxt * KT)
                            else:
                                dve.wait_ge(mid_mm, (nxt + 1) * KT)
                            nc.vector.scalar_tensor_tensor(out=rank_s[:], in0=rank_hi[:].bitcast(F32),
                                                           scalar=negsel[:, 0:1], in1=rank[:], op0=ALU.mult,
                                                           op1=ALU.add).then_inc(rank_done, 1)
                    for m in tile_at(MID_AT, t - 1):
                        dve.wait_ge(gel_done, nxt * KT + m + 1)
                        nc.vector.tensor_tensor(mid_s[:, LO, m], gel[:, m % 2], mid_s[:, HI, m].bitcast(F32),
                                                ALU.subtract).then_inc(mid_done, 1)
                    for m in tile_at(OUT_AT, t):
                        dve.wait_ge(out_mm, nxt * KT + m + 1)
                        if m == 0:
                            need(dve, y_tr, c * JT)
                        nc.vector.scalar_tensor_tensor(out=x1[:, np_, m], in0=act_s[:, LO, m].bitcast(F32), scalar=2.0,
                                                       in1=bulk[:, BANK_OUT[m], :], op0=ALU.mult,
                                                       op1=ALU.add).then_inc(x1_part, 1)
                        dve.wait_ge(x1_part, nxt * KT + m + 1)
                        nc.vector.scalar_tensor_tensor(out=x1[:, np_, m], in0=act_s[:, HI, m].bitcast(F32), scalar=2.0,
                                                       in1=x1[:, np_, m], op0=ALU.mult,
                                                       op1=ALU.add).then_inc(x1_done, 1)
                    for m in tile_at(OUT_AT, t - 1):
                        dve.wait_ge(x1hi_done, nxt * KT + m + 1)
                        nc.vector.tensor_tensor(act_s[:, LO, m], x1[:, np_, m], act_s[:, HI, m].bitcast(F32),
                                                ALU.subtract).then_inc(x1lo_done, 1)

            run_chunks(dve, chunk)

        @block.tensor
        def _(pe):
            pe.wait_ge(pool_set, 3)
            pe.wait_ge(vec_in, 64)
            nc.tensor.transpose(bulk[:, 2, 0:4 * KT], vecs, ident[0:4 * KT, 0:4 * KT]).then_inc(vec_tr, 1)
            pe.wait_ge(chain, 10)
            for k in range(KT):
                nc.tensor.transpose(bulk[:, 0, k * B:(k + 1) * B], cn[:, 1, k * P:(k + 1) * P], ident[0:B, 0:B])
            for k in range(KT):
                last = nc.tensor.transpose(bulk[:, 0, (KT + k) * B:(KT + k + 1) * B], cn[:, 0, k * P:(k + 1) * P],
                                           ident[0:B, 0:B])
            last.then_inc(cond_tr, 1)
            pe.wait_ge(cT_done, 1)
            pe.wait_ge(w1_in, 16)
            w1_v = work[:, RING - 1, :].rearrange("p (k n) -> p k n", k=KT)
            for m in range(KT):
                for k in range(KT):
                    last = nc.tensor.matmul(bulk[:, 1, m * B:(m + 1) * B], w1_v[:, k, m * P:(m + 1) * P], cT[:, k, :],
                                            start=(k == 0), stop=(k == KT - 1))
            last.then_inc(hT_mm, 1)
            pe.wait_ge(stage_in[1], 16)
            for k in range(KT):
                if k >= 2:
                    pe.wait_ge(wsplit, k - 1)
                for n in range(KT):
                    last = nc.tensor.transpose(bulk[:, 4 + k % 2, n * P:(n + 1) * P],
                                               stage[:, 1, n, k * P:(k + 1) * P], ident[:])
                last.then_inc(up_tr, 1)
            pe.wait_ge(wsplit, KT)
            pe.wait_ge(hT_done, 1)

            def turn(n):
                pe.wait_ge(fac_done, n + 1)
                if n >= 2:
                    pe.wait_ge(fac_split, n - 1)
                for g in range(GROUPS):
                    last = nc.tensor.transpose(bulk[:, 4 + n % 2, g * P:(g + 1) * P],
                                               fac[:, n % 2, g].rearrange("p e b r -> p (e b r)"), ident[:])
                last.then_inc(fac_tr, 1)

            def spread(n):
                pe.wait_ge(row_done, 2 * n + 2)
                if n >= 2:
                    pe.wait_ge(fac_done, n - 1)
                wv = wrow[:, n % 2, :].rearrange("b (d r) -> b d r", r=RANK)
                for r in range(RANK):
                    last = nc.tensor.transpose(bulk[:, n % 2, r * B:(r + 1) * B], wv[:, :, r], ident[0:B, 0:B])
                last.then_inc(fac_mm, 1)

            pe.wait_ge(h0_done, 1)
            for n in range(2 * len(W2_TILES)):
                pe.wait_ge(w2_in[n % RING], 16 * (n // RING + 1))
                if n >= 2:
                    pe.wait_ge(row_done, n - 1)
                wv = work[:, n % RING, :].rearrange("p (k n) -> p k n", k=KT)
                for k in range(KT):
                    last = nc.tensor.matmul(bulk[0:B, 2 + n % 2, :], hT[:, k, :], wv[:, k, :],
                                            start=(k == 0), stop=(k == KT - 1))
                last.then_inc(row_mm, 1)
                if n >= 2 and n % 2 == 0:
                    spread(n // 2 - 1)
                if n >= 3 and n % 2 and W2_TILES[n // 2 - 1][0] in (0, 3):
                    turn(n // 2 - 1)
            spread(len(W2_TILES) - 1)
            turn(len(W2_TILES) - 1)
            pe.wait_ge(fac_split, len(W2_TILES))

            def rank_in(out_bank, fac_s, src, k):
                for g in range(GROUPS):
                    for p, (a, w) in enumerate(PASSES):
                        last = nc.tensor.matmul(bulk[:, out_bank, g * GC:(g + 1) * GC], fac_s[:, w, k, g, :],
                                                src[:, a, k, g * GC:(g + 1) * GC], start=(k == g == p == 0),
                                                stop=(k == KT - 1 and p == len(PASSES) - 1), skip_group_check=True)
                return last

            def dense(stage_plan, i, banks, w_s, src, rank_f, done):
                items, _, starts, ends, _ = stage_plan
                m, k, p = items[i]
                if p >= 0:
                    a, w = PASSES[p]
                    mm = nc.tensor.matmul(bulk[:, banks[m], :], w_s[:, w, k, m * P:(m + 1) * P], src[:, a, k, :],
                                          start=(i in starts), stop=(i in ends), skip_group_check=True)
                else:
                    mm = nc.tensor.matmul(bulk[:, banks[m], k * GC:(k + 1) * GC],
                                          rank_f[:, -1 - p, k, m * P:(m + 1) * P], rank_s[:, k * GC:(k + 1) * GC],
                                          start=False, stop=(i in ends), skip_group_check=True)
                if i in ends:
                    mm.then_inc(done, 1)

            def quadrant(fo, fi):
                for m in range(HT):
                    for k in range(fi * HT, (fi + 1) * HT):
                        for q in range(PARTS):
                            n = fo * HT + m
                            last = nc.tensor.matmul(R[fo][:, m, 0:PARTS, :], wh_s[:, q, k, n * P:(n + 1) * P],
                                                    hs[:, k, :, :], start=(m == k == q == 0),
                                                    stop=(k == KT - 1 and q == PARTS - 1), skip_group_check=True)
                return last

            def chunk(c, par, recur=True, bulk_on=True, y_on=True):
                nxt, np_ = c + 1, 1 - par if recur else par
                for t in range(TC):
                    if recur:
                        n = c * TC + t
                        need(pe, h_done, 2 * n - 1)
                        pe.wait_ge(xw_placed, 2 * n + 1)
                        quadrant(0, 0)
                        pe.wait_ge(xw_placed, 2 * n + 2)
                        quadrant(1, 0)
                        need(pe, h_done, 2 * n)
                        quadrant(0, 1).then_inc(rec_mm, 1)
                        quadrant(1, 1).then_inc(rec_mm, 1)
                    if bulk_on and SLOT_XT[0] <= t < SLOT_XT[1]:
                        k = t - SLOT_XT[0]
                        if k == 1:
                            need(pe, xw_done, nxt * KT - 3)
                        if k == 2:
                            need(pe, xw_done, nxt * KT)
                        if k == 3:
                            pe.wait_ge(xlo_done, nxt * KT + 1)
                        for j in range(JT):
                            if k == 0:
                                pe.wait_ge(x_in[j], 16 * JB * (nxt + 1))
                            last = nc.tensor.transpose(bulk[:, BANK_XT[k], j * P:(j + 1) * P],
                                                       xn[:, j, k * P:(k + 1) * P], ident[:])
                        last.then_inc(x_tr, 1)
                    if y_on and SLOT_Y[0] <= t < SLOT_Y[1]:
                        j = t - SLOT_Y[0]
                        if j == 0:
                            pe.wait_ge(sum_done, c * TC)
                            if recur:
                                pe.wait_ge(xw_done, c * KT + 2)
                        if j == 2 and bulk_on:
                            pe.wait_ge(xlo_done, nxt * KT + 2)
                        if j == 3:
                            pe.wait_ge(y_done, (c - 1) * JT + 1)
                        for k in range(KT):
                            last = nc.tensor.transpose(bulk[:, BANK_Y[j], k * P:(k + 1) * P],
                                                       x1[:, 1 - par, k, j * P:(j + 1) * P], ident[:])
                        last.then_inc(y_tr, 1)
                    if not bulk_on:
                        continue
                    if SLOT_U[0] <= t < SLOT_U[1]:
                        k = t - SLOT_U[0]
                        pe.wait_ge(xlo_done, nxt * KT + k + 1)
                        last = rank_in(BANK_U, a2_s, act_s, k)
                        if k == KT - 1:
                            last.then_inc(u_mm, 1)
                    if SLOT_MID[0] <= t < SLOT_MID[1]:
                        for i in range(*MID[1][t - SLOT_MID[0]]):
                            m, _, p = MID[0][i]
                            if i in MID[2] and m in (1, 3) and y_on:
                                pe.wait_ge(y_done, (c - 1) * JT + (2 if m == 1 else 3))
                            if p == -1 and m == 0:
                                pe.wait_ge(rank_done, 2 * nxt + 1)
                            dense(MID, i, BANK_MID, down_s, act_s, b2_s, mid_mm)
                    if SLOT_V[0] <= t < SLOT_V[1]:
                        if t == SLOT_V[0] and y_on:
                            pe.wait_ge(y_done, c * JT)
                        for k in (2 * (t - SLOT_V[0]), 2 * (t - SLOT_V[0]) + 1):
                            pe.wait_ge(mid_done, nxt * KT + k + 1)
                            last = rank_in(BANK_V, b1_s, mid_s, k)
                        if t == SLOT_V[1] - 1:
                            last.then_inc(v_mm, 1)
                    if SLOT_OUT[0] <= t < SLOT_OUT[1]:
                        for i in range(*OUT[1][t - SLOT_OUT[0]]):
                            m, _, p = OUT[0][i]
                            if i == 0:
                                pe.wait_ge(rank_sel, 2 * nxt + 1)
                            if p == -1 and m == 0:
                                pe.wait_ge(rank_done, 2 * nxt + 2)
                            dense(OUT, i, BANK_OUT, up_s, mid_s, a1_s, out_mm)
                    if SLOT_XW[0] <= t < SLOT_XW[1]:
                        for i in range(*XW[1][t - SLOT_XW[0]]):
                            m, k, p = XW[0][i]
                            if p == 0 and m == 0:
                                pe.wait_ge(x1lo_done, nxt * KT + k + 1)
                            dense(XW, i, BANK_XW, wx_s, act_s, None, xw_mm)

            run_chunks(pe, chunk)


_INS = ["x", "cond_1024", "L0_cond_base_down", "L0_cond_base_up", "L0_cond_ln_gamma", "L0_cond_ln_beta", "L0_cond_W1",
        "L0_cond_bias1", "L0_cond_W2", "L0_cond_bias2", "L1_cond_Wx", "L1_cond_Wh", "L1_cond_b"]


def kernel(**inputs):
    import numpy as _np
    import concourse.bacc as _bacc
    from concourse import mybir as _mybir
    from concourse.bass_utils import run_bass_kernel_spmd as _run

    nc = _bacc.Bacc("TRN2", target_bir_lowering=False, num_devices=1)
    arrays, args = {}, []
    for name in _INS:
        a = _np.ascontiguousarray(inputs[name])
        arrays[f"in_{name}_dram"] = a
        args.append(nc.dram_tensor(f"in_{name}_dram", a.shape, _mybir.dt.from_np(a.dtype), kind="ExternalInput").ap())
    out = nc.dram_tensor("out_0_dram", inputs["x"].shape, _mybir.dt.float32, kind="ExternalOutput").ap()
    build(nc, *args, out)
    r = _run(nc, [arrays], core_ids=[0])
    return r.results[0]["out_0_dram"]
```

```python
from contextlib import ExitStack

import concourse.bass as bass
from concourse import mybir

P = 128
F32 = mybir.dt.float32
F32R = mybir.dt.float32r
F16 = mybir.dt.float16
U32 = mybir.dt.uint32
ALU = mybir.AluOpType
ACT = mybir.ActivationFunctionType
AX = mybir.AxisListType

RANK = 8
LN_EPS = 1e-5
PARTS = 2
H_SCALE = 2.0 ** 15
W_TOP = 2.0 ** 14
W_LEAST = 2.0 ** -26
GROUPS = 2
REPS = 2
HI, LO = 0, 1
PASSES = ((HI, HI), (HI, LO), (LO, HI))
BULK_BANKS = 6
IDLE_MM = 3

BANK_XT = (0, 1, 3, 4)
BANK_Y = (2, 5, 0, 1)
BANK_U = 2
BANK_MID = (3, 4, 5, 0)
BANK_V = 1
BANK_OUT = (2, 3, 4, 5)
BANK_XW = (0, 1, 2, 3)


def portions(costs, shares):
    total, out, i, at = sum(costs), [], 0, 0.0
    for n in range(len(shares)):
        first, end = i, total * sum(shares[:n + 1]) / sum(shares)
        while i < len(costs) and at + costs[i] / 2 <= end:
            at += costs[i]
            i += 1
        out.append((first, i if n < len(shares) - 1 else len(costs)))
    return out


def dense_items(kt, rank):
    main = [[(m, k, p) for k in range(kt) for p in range(len(PASSES))] for m in range(kt)]
    low = [[(m, g, -1 - w) for g in range(GROUPS) for w in (HI, LO)] for m in range(kt)]
    if rank:
        items = main[0] + main[1][:6] + low[0] + main[1][6:] + low[1]
    else:
        items = main[0][:9] + main[1][:9] + main[0][9:] + main[1][9:]
    for m in range(2, kt):
        items += main[m] + (low[m] if rank else [])
    return items


XT_SLOT = (0, 0, 1, 1)
Y_SLOT = (0, 1, 2, 2)
U_SLOT = (2, 3, 3, 4)
V_SLOT = (14, 14, 15, 15)
MID_SLOTS = (4, (0.5,) + (1,) * 9)
OUT_SLOTS = (16, (1,) * 9)
XW_SLOTS = (25, (1,) * 6 + (0.7,))
XLO_AT = (0, 1, 2, 3)
XALL_AT = (6, 7, 9, 11)
WH_MAX, WH_SCALES, WH_SPREAD, WH_HI, WH_LO = 17, 20, 21, 23, 25


def build(nc: bass.Bass, x, cond, down, up, gamma, beta, w1, bias1, w2, bias2, wx, wh, b, y):
    B, T, D = x.shape
    KT = D // P
    TC = 512 // B
    NC = T // TC
    HT = KT // 2
    COLS = B * TC
    JB = P // TC
    JT = B // JB
    GB = B // GROUPS
    GC = GB * TC
    QUARTER = D * RANK
    W2C = P * RANK
    HALVES = 2 * 4 * KT
    assert COLS == 512 and GB * RANK * REPS == P and NC % 2 == 0 and KT == JT == 4 and TC == 32

    with ExitStack() as ctx:
        def sb(name, shape, dt=F32):
            return ctx.enter_context(nc.sbuf_tensor(name, shape, dt))

        def psum(name, shape, dt=F32):
            return ctx.enter_context(nc.psum_tensor(name, shape, dt))

        def sem(name):
            return ctx.enter_context(nc.semaphore(name))

        down_s = sb("down_s", [P, 2, KT, D], F32R)
        up_s = sb("up_s", [P, 2, KT, D], F32R)
        wx_s = sb("wx_s", [P, 2, KT, D], F32R)
        wh_s = sb("wh_s", [P, PARTS, KT, D], F16)
        a2_s = sb("a2_s", [P, 2, KT, GROUPS, P], F32R)
        b1_s = sb("b1_s", [P, 2, KT, GROUPS, P], F32R)
        b2_s = sb("b2_s", [P, 2, GROUPS, D], F32R)
        a1_s = sb("a1_s", [P, 2, GROUPS, D], F32R)

        RING = 4
        work = sb("work", [P, RING + 2, KT * 512])
        x1 = work[:, 0:2, :].rearrange("p s (k n) -> p s k n", k=KT)
        xw = work[:, 2:4, :].rearrange("p s (k n) -> p s k n", k=KT)
        xn = work[:, 4, :].rearrange("p (j n) -> p j n", j=JT)
        yn = work[:, 5, :].rearrange("p (j n) -> p j n", j=JT)
        stage = sb("stage", [P, 2, KT, D])
        act_s = sb("act_s", [P, 2, KT, COLS], F32R)
        mid_s = sb("mid_s", [P, 2, KT, COLS], F32R)
        gel = sb("gel", [P, 2, COLS])
        rank = sb("rank", [P, COLS])
        rank_hi = sb("rank_hi", [P, COLS], F32R)
        rank_s = sb("rank_s", [P, COLS], F32R)
        mask = sb("mask", [P, COLS], U32)
        mask_b = sb("mask_b", [P, 2, GB])
        mask_i = sb("mask_i", [P, GB], U32)
        negsel = sb("negsel", [P, 1])
        ident = sb("ident", [P, P])
        z = sb("z", [P, KT, B])
        hf = sb("hf", [P, 4, KT, B])
        hs = sb("hs", [P, KT, PARTS, B], F16)
        seen = sb("seen", [P, 1])
        h0s = sb("h0s", [P, KT, PARTS, B])
        wmax = sb("wmax", [P, 3])
        top = sb("top", [1, 2])
        exp_bits = sb("exp_bits", [1, 1])
        top_i = sb("top_i", [1, 1], U32)
        sc1 = sb("sc1", [1, 3])
        ones = sb("ones", [1, P])
        scl = sb("scl", [P, 3])
        w_scale, fwd, inv = scl[:, 0:1], scl[:, 1:2], scl[:, 2:3]
        bs = sb("bs", [P, KT])
        w2_s = (act_s, mid_s)
        w1_f = work[:, RING, :].rearrange("p (k n) -> p k n", k=KT)
        wrow = work[0:2 * B, 5, :].rearrange("b (s n) -> b s n", s=2)
        cn = work[0:B, 5, 0:2 * D].rearrange("b (s d) -> b s d", s=2)
        vecs = work[0:4 * KT, 5, 2 * D:2 * D + P]
        ln = sb("ln", [B, 8])
        cT = sb("cT", [P, KT, B])
        hT = sb("hT", [P, KT, B])
        h_s = sb("h_s", [P, KT, 2, B], F32R)
        fold = sb("fold", [2 * B, B])
        vT = sb("vT", [P, 4, KT])
        bias2T = sb("bias2T", [P, 4, KT, RANK])
        fac = sb("fac", [P, 2, GROUPS, REPS, GB, RANK])

        rec = psum("rec", [P, 2, 512])
        R = [rec[:, f, 0:HT * (PARTS + 1) * B].rearrange("p (m j b) -> p m j b", m=HT, j=PARTS + 1) for f in range(2)]
        bulk = psum("bulk", [P, BULK_BANKS, 512])

        cond_in = sem("cond_in")
        vec_in = sem("vec_in")
        vec_tr = sem("vec_tr")
        vT_done = sem("vT_done")
        small_in = sem("small_in")
        w1_in = sem("w1_in")
        stage_in = [sem(f"stage_in{i}") for i in range(2)]
        w2_in = [sem(f"w2_in{i}") for i in range(RING)]
        x_in = [sem(f"x_in{j}") for j in range(JT)]
        y_out = [sem(f"y_out{j}") for j in range(JT)]
        pool_set = sem("pool_set")
        chain = sem("chain")
        sqrt_done = sem("sqrt_done")
        cond_tr = sem("cond_tr")
        cT_done = sem("cT_done")
        hT_mm = sem("hT_mm")
        hT_done = sem("hT_done")
        up_tr = sem("up_tr")
        up_split = sem("up_split")
        w_hi = sem("w_hi")
        w_split = sem("w_split")
        wmax_done = sem("wmax_done")
        wmax_tr = sem("wmax_tr")
        sc1_done = sem("sc1_done")
        scl_mm = sem("scl_mm")
        scl_done = sem("scl_done")
        wh_hi = sem("wh_hi")
        wh_split = sem("wh_split")
        fold_set = sem("fold_set")
        h_split = sem("h_split")
        w2_hi = sem("w2_hi")
        w2_lo = sem("w2_lo")
        row_hi = sem("row_hi")
        row_mm = sem("row_mm")
        row_done = sem("row_done")
        fac_mm = sem("fac_mm")
        fac_done = sem("fac_done")
        fac_tr = sem("fac_tr")
        fac_split = sem("fac_split")
        y_tr = sem("y_tr")
        x_tr = sem("x_tr")
        u_mm = sem("u_mm")
        mid_mm = sem("mid_mm")
        v_mm = sem("v_mm")
        out_mm = sem("out_mm")
        xw_mm = sem("xw_mm")
        rec_mm = sem("rec_mm")
        y_done = sem("y_done")
        xhi_done = sem("xhi_done")
        xlo_done = sem("xlo_done")
        rank_sel = sem("rank_sel")
        rank_rnd = sem("rank_rnd")
        rank_done = sem("rank_done")
        gel_done = sem("gel_done")
        mid_done = sem("mid_done")
        x_all = sem("x_all")
        x1_done = sem("x1_done")
        x1hi_done = sem("x1hi_done")
        x1lo_done = sem("x1lo_done")
        xw_done = sem("xw_done")
        z_done = sem("z_done")
        tanh_done = sem("tanh_done")
        hi_done = sem("hi_done")
        h_done = sem("h_done")
        xw_placed = sem("xw_placed")
        sum_done = sem("sum_done")

        w2_v = w2.rearrange("(k p) n -> p k n", p=P)
        W2_TILES = [(q, dt) for q in (2, 3, 1, 0) for dt in range(KT)]
        LAST = len(W2_TILES) - 1

        def turned(n):
            return rec[:, n % 2, 512 - GROUPS * P:512]

        def need(eng, s, n):
            if not isinstance(n, int) or n > 0:
                eng.wait_ge(s, n)

        def dma_x(eng, c, j):
            eng.dma_start(xn[:, j, :], x[j * JB:(j + 1) * JB, bass.ds(c * TC, TC), :]).then_inc(x_in[j], 16)

        block = ctx.enter_context(nc.Block())

        def plan(rank, first, shares):
            items = dense_items(KT, rank)
            parts = portions([1 if p >= 0 else 0.5 for _, _, p in items], shares)
            ends = {max(i for i, it in enumerate(items) if it[0] == m): m for m in range(KT)}
            starts = {min(i for i, it in enumerate(items) if it[0] == m): m for m in range(KT)}
            at = {m: first + next(n for n, (a, z) in enumerate(parts) if a <= i < z) for i, m in ends.items()}
            by_slot = {first + n: range(*part) for n, part in enumerate(parts)}
            return items, by_slot, starts, ends, at

        MID, OUT, XW = plan(True, *MID_SLOTS), plan(True, *OUT_SLOTS), plan(False, *XW_SLOTS)
        MID_AT, OUT_AT, XW_AT = MID[-1], OUT[-1], XW[-1]

        def tile_at(at, t):
            return [m for m in range(KT) if at[m] == t]

        def run_chunks(eng, chunk):
            chunk(-1, 0, recur=False, y_on=False)
            chunk(0, 0, y_on=False)
            with eng.Fori(0, (NC - 2) // 2) as i:
                chunk(i * 2 + 1, 1)
                chunk(i * 2 + 2, 0)
            chunk(NC - 1, 1, bulk_on=False)
            chunk(NC, 0, recur=False, bulk_on=False)

        @block.sync
        def _(sp):
            sp.dma_start(cn[:, 0, :], cond).then_inc(cond_in, 16)
            for v, vec in enumerate((gamma, beta, bias1, b)):
                sp.dma_start(vecs[v * KT:(v + 1) * KT, :], vec.rearrange("(k p) -> k p", p=P)).then_inc(vec_in, 16)
            for q in range(4):
                sp.dma_start(bias2T[:, q], bias2[q * QUARTER:(q + 1) * QUARTER].rearrange(
                    "(k p r) -> p k r", p=P, r=RANK)).then_inc(small_in, 16)
            sp.dma_start(w1_f, w1.rearrange("(k p) n -> p k n", p=P)).then_inc(w1_in, 16)

            def load_w2(n):
                q, dt = W2_TILES[n // 2]
                if n >= RING:
                    sp.wait_ge(w2_lo, n - RING + 1)
                c0 = q * QUARTER + dt * W2C + n % 2 * 512
                sp.dma_start(work[:, n % RING, :].rearrange("p (k n) -> p k n", k=KT),
                             w2_v[:, :, c0:c0 + 512]).then_inc(w2_in[n % RING], 16)

            def load_w(slot, w):
                sp.dma_start(stage[:, slot], w.rearrange("(k p) n -> p k n", p=P)).then_inc(stage_in[slot], 16)

            for n in range(RING):
                load_w2(n)
            load_w(1, up)
            for n in range(RING, RING + 2):
                load_w2(n)
            load_w(0, down)
            for n in range(RING + 2, HALVES - RING):
                load_w2(n)
            sp.wait_ge(hT_mm, 1)
            for j in range(JT):
                dma_x(sp, 0, j)
            for n in range(HALVES - RING, HALVES):
                load_w2(n)
            sp.wait_ge(w_split, 1)
            load_w(0, wx)
            sp.wait_ge(up_tr, KT)
            load_w(1, wh)

            def next_x(c):
                sp.wait_ge(x_tr, c * KT)
                for j in range(JT):
                    dma_x(sp, c, j)

            def store_y(c):
                for j in range(JT):
                    sp.wait_ge(y_done, c * JT + j + 1)
                    sp.dma_start(y[j * JB:(j + 1) * JB, bass.ds(c * TC, TC), :], yn[:, j, :]).then_inc(y_out[j], 16)

            next_x(1)
            next_x(2)
            with sp.Fori(0, NC - 3) as c:
                next_x(c + 3)
                store_y(c)
            for c in range(NC - 3, NC):
                store_y(c)
            for j in range(JT):
                sp.wait_ge(y_out[j], 16 * NC)

        @block.gpsimd
        def _(pool):
            nc.gpsimd.memset(ident[:], 0.0).then_inc(pool_set, 1)
            nc.gpsimd.memset(mask_b[:], 1.0).then_inc(pool_set, 1)
            pool.wait_ge(pool_set, 2)
            nc.gpsimd.affine_select(out=ident[:], in_=ident[:], compare_op=ALU.not_equal, fill=1.0, base=0,
                                    pattern=[[-1, P]], channel_multiplier=1).then_inc(pool_set, 1)
            for rep in range(REPS):
                m = mask_b[:, rep, :]
                base = -rep * GB * RANK
                nc.gpsimd.affine_select(out=m, in_=m, compare_op=ALU.is_ge, fill=0.0, base=base,
                                        pattern=[[-RANK, GB]], channel_multiplier=1).then_inc(pool_set, 1)
                pool.wait_ge(pool_set, 4 + 2 * rep)
                nc.gpsimd.affine_select(out=m, in_=m, compare_op=ALU.is_ge, fill=0.0, base=RANK - 1 - base,
                                        pattern=[[RANK, GB]], channel_multiplier=-1).then_inc(pool_set, 1)

            for n, dst in enumerate((down_s, wx_s)):
                pool.wait_ge(w_hi, n + 1)
                nc.gpsimd.tensor_tensor(dst[:, LO], stage[:, 0], dst[:, HI].bitcast(F32),
                                        ALU.subtract).then_inc(w_split, 1)
            def chunk(c, par, recur=True, bulk_on=True, y_on=True):
                if not recur:
                    return
                for t in range(TC):
                    n = c * TC + t
                    if t == 0:
                        need(pool, x1lo_done, (c + 1) * KT)
                    pool.wait_ge(tanh_done, 2 * n + 2)
                    xs = x1[:, par].rearrange("p k (b t) -> p k b t", t=TC)[:, :, :, t]
                    nc.gpsimd.tensor_tensor(xs, xs, hf[:, t % 4], ALU.add).then_inc(sum_done, 1)

            run_chunks(pool, chunk)

        @block.scalar
        def _(act):
            act.wait_ge(chain, 5)
            nc.scalar.activation(ln[:, 4:5], ln[:, 3:4], ACT.Sqrt).then_inc(sqrt_done, 1)

            def w2_high(n):
                act.wait_ge(w2_in[n % RING], 16 * (n // RING + 1))
                if n >= 2:
                    act.wait_ge(row_hi, n - 1)
                    act.wait_ge(w2_lo, n - 1)
                nc.scalar.copy(w2_s[n % 2][:, HI].rearrange("p k n -> p (k n)"), work[:, n % RING, :]).then_inc(w2_hi, 1)

            w2_high(0)
            w2_high(1)
            act.wait_ge(hT_mm, 1)
            act.wait_ge(vT_done, 1)
            for m in range(KT):
                h1 = bulk[:, 1, m * B:(m + 1) * B]
                nc.scalar.activation(hT[:, m, :], h1, ACT.Gelu, bias=vT[:, 2, m:m + 1])
                last = nc.scalar.activation(h_s[:, m, HI, :], h1, ACT.Gelu, bias=vT[:, 2, m:m + 1])
            last.then_inc(hT_done, 1)
            for n in range(HALVES):
                if n + 2 < HALVES:
                    w2_high(n + 2)
                act.wait_ge(row_mm, n + 1)
                if n >= 4:
                    act.wait_ge(fac_mm, n // 2 - 1)
                nc.scalar.copy(wrow[:, n // 2 % 2, n % 2 * 512:n % 2 * 512 + 512],
                               bulk[0:2 * B, 2 + n % 2, :]).then_inc(row_done, 1)
                if n == RING + 2:
                    act.wait_ge(stage_in[0], 16)
                    nc.scalar.copy(down_s[:, HI], stage[:, 0]).then_inc(w_hi, 1)

            def place(par, t, f):
                nc.scalar.activation(R[f][:, :, PARTS, :],
                                     xw[:, par].rearrange("p k (b t) -> p k b t", t=TC)[:, f * HT:(f + 1) * HT, :, t],
                                     ACT.Copy).then_inc(xw_placed, 1)

            def chunk(c, par, recur=True, bulk_on=True, y_on=True):
                nxt, np_ = c + 1, 1 - par if recur else par
                for t in range(TC):
                    for f in range(2) if recur else ():
                        n = c * TC + t
                        half = slice(f * HT, (f + 1) * HT)
                        act.wait_ge(z_done, 2 * n + f + 1)
                        if f == 0 and not (isinstance(n, int) and n < 4):
                            act.wait_ge(sum_done, n - 3)
                        nc.scalar.activation(hf[:, t % 4, half], z[:, half], ACT.Tanh, scale=inv).then_inc(tanh_done, 1)
                    for f in range(2) if recur and t + 1 < TC else ():
                        if t == 0 and f == 1:
                            act.wait_ge(xw_done, (c + 1) * KT)
                        place(par, t + 1, f)
                    for k in tile_at(XT_SLOT, t) if bulk_on else ():
                        act.wait_ge(x_tr, nxt * KT + k + 1)
                        if k == 0:
                            need(act, xw_mm, nxt * KT)
                        nc.scalar.copy(act_s[:, HI, k], bulk[:, BANK_XT[k], :]).then_inc(xhi_done, 1)
                    for j in tile_at(Y_SLOT, t - 1) if y_on else ():
                        act.wait_ge(y_tr, (c - 1) * JT + j + 1)
                        nc.scalar.copy(yn[:, j, :], bulk[:, BANK_Y[j], :]).then_inc(y_done, 1)
                    if y_on and recur and t == TC - 1:
                        for j in range(JT):
                            act.wait_ge(y_out[j], 16 * c)
                    if not bulk_on:
                        continue
                    if not recur and t == MID_AT[0] - 1:
                        act.wait_ge(stage_in[0], 32)
                        nc.scalar.copy(wx_s[:, HI], stage[:, 0]).then_inc(w_hi, 1)
                    if not recur and t == WH_HI:
                        act.wait_ge(scl_done, 1)
                        nc.scalar.activation(wh_s[:, 0], stage[:, 1], ACT.Identity, scale=w_scale).then_inc(wh_hi, 1)
                    for m in tile_at(MID_AT, t):
                        act.wait_ge(mid_mm, nxt * KT + m + 1)
                        need(act, mid_done, nxt * KT + m - 1)
                        if m == 0:
                            need(act, out_mm, nxt * KT)
                        nc.scalar.activation(gel[:, m % 2], bulk[:, BANK_MID[m], :], ACT.Gelu)
                        nc.scalar.activation(mid_s[:, HI, m], bulk[:, BANK_MID[m], :],
                                             ACT.Gelu).then_inc(gel_done, 1)
                    for m in tile_at(OUT_AT, t - 1):
                        act.wait_ge(x1_done, nxt * KT + m + 1)
                        nc.scalar.copy(act_s[:, HI, m], x1[:, np_, m]).then_inc(x1hi_done, 1)
                    for m in tile_at(XW_AT, t):
                        if m == KT - 1:
                            continue
                        act.wait_ge(xw_mm, nxt * KT + m + 1)
                        nc.scalar.activation(xw[:, np_, m], bulk[:, BANK_XW[m], :], ACT.Identity,
                                             bias=bs[:, m:m + 1], scale=fwd).then_inc(xw_done, 1)
                if bulk_on:
                    if recur:
                        act.wait_ge(z_done, 2 * TC * (c + 1) - 1)
                    act.wait_ge(xw_done, nxt * KT + KT - 1)
                    place(np_, 0, 0)
                    if recur:
                        act.wait_ge(z_done, 2 * TC * (c + 1))
                    m = KT - 1
                    nc.scalar.activation(R[1][:, 0:HT - 1, PARTS, :], xw[:, np_].rearrange(
                        "p k (b t) -> p k b t", t=TC)[:, HT:m, :, 0], ACT.Copy)
                    act.wait_ge(xw_mm, nxt * KT + KT)
                    nc.scalar.activation(R[1][:, HT - 1, PARTS, :], bulk[:, BANK_XW[m], :].rearrange(
                        "p (b t) -> p b t", t=TC)[:, :, 0], ACT.Identity, bias=bs[:, m:m + 1],
                                         scale=fwd).then_inc(xw_placed, 1)
                    nc.scalar.activation(xw[:, np_, m], bulk[:, BANK_XW[m], :], ACT.Identity,
                                         bias=bs[:, m:m + 1], scale=fwd).then_inc(xw_done, 1)

            run_chunks(act, chunk)

        @block.vector
        def _(dve):
            links = [0]

            def link(ins):
                links[0] += 1
                ins.then_inc(chain, 1)
                dve.wait_ge(chain, links[0])

            dve.wait_ge(cond_in, 16)
            link(nc.vector.tensor_reduce(ln[:, 0:1], cn[:, 0, :], AX.X, ALU.add))
            link(nc.vector.tensor_scalar(ln[:, 1:2], ln[:, 0:1], 1.0 / D, None, ALU.mult))
            link(nc.vector.tensor_scalar(cn[:, 1, :], cn[:, 0, :], ln[:, 1:2], None, ALU.subtract))
            link(nc.vector.tensor_tensor_reduce(out=gel[0:B, 0, :], in0=cn[:, 1, :], in1=cn[:, 1, :], scale=1.0,
                                                scalar=0.0, op0=ALU.mult, op1=ALU.add, accum_out=ln[:, 2:3]))
            link(nc.vector.tensor_scalar(ln[:, 3:4], ln[:, 2:3], 1.0 / D, LN_EPS, ALU.mult, ALU.add))
            dve.wait_ge(sqrt_done, 1)
            link(nc.vector.reciprocal(ln[:, 5:6], ln[:, 4:5]))
            link(nc.vector.tensor_scalar(ln[:, 6:7], ln[:, 5:6], ln[:, 5:6], ln[:, 3:4], ALU.mult, ALU.mult))
            link(nc.vector.tensor_scalar(ln[:, 7:8], ln[:, 6:7], -0.5, 1.5, ALU.mult, ALU.add))
            link(nc.vector.tensor_scalar(ln[:, 6:7], ln[:, 7:8], ln[:, 5:6], None, ALU.mult))
            link(nc.vector.tensor_scalar(cn[:, 1, :], cn[:, 1, :], ln[:, 6:7], None, ALU.mult))
            dve.wait_ge(vec_tr, 1)
            nc.vector.tensor_copy(vT[:], bulk[:, 2, 0:4 * KT].rearrange("p (v k) -> p v k", v=4)).then_inc(vT_done, 1)
            dve.wait_ge(cond_tr, 1)
            dve.wait_ge(vT_done, 1)
            dve.wait_ge(small_in, 64)
            for k in range(KT):
                last = nc.vector.tensor_scalar(cT[:, k, :], bulk[:, 0, k * B:(k + 1) * B], vT[:, 0, k:k + 1],
                                               vT[:, 1, k:k + 1], ALU.mult, ALU.add)
            last.then_inc(cT_done, 1)
            h0 = bulk[:, 0, KT * B:2 * KT * B].rearrange("p (k b) -> p k b", k=KT)
            nc.vector.memset(h0s[:], 0.0)
            nc.vector.memset(ones[:], 1.0)
            nc.vector.memset(sc1[:], 0.0)
            link(nc.vector.memset(exp_bits[:], float("inf")))
            nc.vector.tensor_copy(h0s[:, :, 0, :], h0)

            nc.vector.memset(negsel[0:P // 2, :], 0.0)
            nc.vector.memset(negsel[P // 2:P, :], -1.0)
            nc.vector.memset(rank[:], 0.0)
            dve.wait_ge(pool_set, 7)
            nc.vector.tensor_tensor(fold[:], ident[0:2 * B, 0:B], ident[0:2 * B, B:2 * B], ALU.add).then_inc(fold_set, 1)
            link(nc.vector.tensor_tensor(mask_i[:], mask_b[:, 0, :], mask_b[:, 1, :], ALU.add))
            mv = mask[:].rearrange("p (g b t) -> p g b t", g=GROUPS, t=TC)
            for g in range(GROUPS):
                last = nc.vector.tensor_copy(mv[:, g], mask_i[:].rearrange("p (b o) -> p b o", o=1)
                                             .broadcast_to([P, GB, TC]))
            link(last)

            def w2_low(n):
                dve.wait_ge(w2_hi, n + 1)
                if n >= 2:
                    dve.wait_ge(row_mm, n - 1)
                dst = w2_s[n % 2].rearrange("p s k n -> p s (k n)")
                nc.vector.tensor_tensor(dst[:, LO], work[:, n % RING, :], dst[:, HI].bitcast(F32),
                                        ALU.subtract).then_inc(w2_lo, 1)

            def split_up(k):
                dve.wait_ge(up_tr, k + 1)
                src = bulk[:, 4 + k % 2, :]
                link(nc.vector.tensor_copy(up_s[:, HI, k], src))
                nc.vector.tensor_tensor(up_s[:, LO, k], src, up_s[:, HI, k].bitcast(F32),
                                        ALU.subtract).then_inc(up_split, 1)

            def factor(n):
                q, dt = W2_TILES[n]
                f = fac[:, n % 2]
                dve.wait_ge(fac_mm, n + 1)
                if n >= 2:
                    dve.wait_ge(fac_split, n - 1)
                pw = rec[:, n % 2, 0:RANK * B].rearrange("p (r g b) -> p g b r", r=RANK, g=GROUPS)
                bias = bias2T[:, q, dt:dt + 1, :].broadcast_to([P, GB, RANK])
                for rep in range(REPS):
                    for g in range(GROUPS):
                        last = nc.vector.tensor_tensor(f[:, g, rep], pw[:, g], bias, ALU.add)
                last.then_inc(fac_done, 1)

            def split_factor(n):
                q, dt = W2_TILES[n]
                if q in (1, 2):
                    dst = (b1_s if q == 1 else a2_s)[:, :, dt].rearrange("p s g n -> p s (g n)")
                    src = fac[:, n % 2].rearrange("p g e b r -> p (g e b r)")
                    dve.wait_ge(fac_done, n + 1)
                else:
                    dst = (a1_s if q == 0 else b2_s)[:, :, :, dt * P:(dt + 1) * P]
                    src = turned(n).rearrange("p (g n) -> p g n", g=GROUPS)
                    dve.wait_ge(fac_tr, (n % 8) - 3 if n < 8 else (n - 12) + 5)
                link(nc.vector.tensor_copy(dst[:, HI], src))
                nc.vector.tensor_tensor(dst[:, LO], src, dst[:, HI].bitcast(F32), ALU.subtract).then_inc(fac_split, 1)

            w2_low(0)
            dve.wait_ge(hT_done, 1)
            nc.vector.tensor_tensor(h_s[:, :, LO, :], hT[:], h_s[:, :, HI, :].bitcast(F32),
                                    ALU.subtract).then_inc(h_split, 1)
            for n in range(1, HALVES):
                w2_low(n)
                if RING < n <= RING + KT:
                    split_up(n - RING - 1)
                if n >= 4 and n % 2 == 0:
                    factor(n // 2 - 2)
                if n >= 5 and n % 2:
                    split_factor(n // 2 - 2)

            def chunk(c, par, recur=True, bulk_on=True, y_on=True):
                nxt, np_ = c + 1, 1 - par if recur else par
                for t in range(TC):
                    if recur:
                        n = c * TC + t
                        for f in range(2):
                            dve.wait_ge(rec_mm, 2 * n + f + 1)
                            nc.vector.tensor_reduce(z[:, f * HT:(f + 1) * HT], R[f].rearrange("p m j b -> p m b j"),
                                                    AX.X, ALU.add).then_inc(z_done, 1)
                        for f in range(2):
                            half = slice(f * HT, (f + 1) * HT)
                            dve.wait_ge(tanh_done, 2 * n + f + 1)
                            nc.vector.tensor_scalar(hs[:, half, 0, :], hf[:, t % 4, half], H_SCALE, None,
                                                    ALU.mult).then_inc(hi_done, 1)
                            dve.wait_ge(hi_done, 2 * n + f + 1)
                            nc.vector.scalar_tensor_tensor(out=hs[:, half, 1, :], in0=hf[:, t % 4, half],
                                                           scalar=H_SCALE, in1=hs[:, half, 0, :], op0=ALU.mult,
                                                           op1=ALU.subtract).then_inc(h_done, 1)
                    if not bulk_on:
                        continue
                    for k in tile_at(XLO_AT, t):
                        dve.wait_ge(xhi_done, nxt * KT + k + 1)
                        nc.vector.tensor_tensor(act_s[:, LO, k], bulk[:, BANK_XT[k], :],
                                                act_s[:, HI, k].bitcast(F32), ALU.subtract).then_inc(xlo_done, 1)
                    if not recur and t == 0:
                        factor(LAST - 1)
                    if not recur and t == U_SLOT[-1] - 1:
                        split_factor(LAST - 1)
                        factor(LAST)
                    if not recur and t == U_SLOT[-1] + 1:
                        split_factor(LAST)
                    if not recur and t == WH_MAX:
                        dve.wait_ge(stage_in[1], 32)
                        w_rows = stage[:, 1].rearrange("p k n -> p (k n)")
                        link(nc.vector.tensor_reduce(wmax[:, 0:1], w_rows, AX.X, ALU.max))
                        link(nc.vector.tensor_reduce(wmax[:, 1:2], w_rows, AX.X, ALU.min))
                        nc.vector.scalar_tensor_tensor(out=wmax[:, 2:3], in0=wmax[:, 1:2], scalar=-1.0,
                                                       in1=wmax[:, 0:1], op0=ALU.mult,
                                                       op1=ALU.max).then_inc(wmax_done, 1)
                    if not recur and t == WH_SCALES:
                        dve.wait_ge(wmax_tr, 1)
                        link(nc.vector.tensor_reduce(top[:, 0:1], rec[0:1, 0, 0:P], AX.X, ALU.max))
                        link(nc.vector.tensor_scalar(top[:, 1:2], top[:, 0:1], W_LEAST, None, ALU.max))
                        link(nc.vector.tensor_tensor(top_i[:], top[:, 1:2].bitcast(U32), exp_bits[:].bitcast(U32),
                                                     ALU.bitwise_and))
                        link(nc.vector.tensor_scalar(sc1[:, 2:3], top_i[:].bitcast(F32), 1 / (W_TOP * H_SCALE),
                                                     None, ALU.mult))
                        link(nc.vector.reciprocal(sc1[:, 1:2], sc1[:, 2:3]))
                        nc.vector.tensor_scalar(sc1[:, 0:1], sc1[:, 1:2], 1 / H_SCALE, None, ALU.mult).then_inc(sc1_done, 1)
                    if not recur and t == WH_SPREAD:
                        dve.wait_ge(scl_mm, 1)
                        link(nc.vector.tensor_copy(scl[:], rec[:, 1, 0:3]))
                        nc.vector.tensor_scalar(h0s[:, :, 0, :], h0s[:, :, 0, :], fwd, None, ALU.mult)
                        nc.vector.tensor_scalar(bs[:], vT[:, 3, :], fwd, None, ALU.mult).then_inc(scl_done, 1)
                    if not recur and t == WH_LO:
                        dve.wait_ge(wh_hi, 1)
                        nc.vector.scalar_tensor_tensor(out=wh_s[:, 1], in0=stage[:, 1], scalar=w_scale,
                                                       in1=wh_s[:, 0], op0=ALU.mult,
                                                       op1=ALU.subtract).then_inc(wh_split, 1)
                    for e, last_slot, mm, bank in ((0, U_SLOT[-1], u_mm, BANK_U), (1, V_SLOT[-1], v_mm, BANK_V)):
                        if t == last_slot:
                            dve.wait_ge(mm, nxt + 1)
                            nc.vector.tensor_copy(seen[:], bulk[:, bank, 0:1])
                            nc.vector.copy_predicated(rank[:], mask[:], bulk[:, bank, :]).then_inc(rank_sel, 1)
                        if t == last_slot + 1:
                            dve.wait_ge(rank_sel, 2 * nxt + e + 1)
                            nc.vector.tensor_copy(rank_hi[:], rank[:]).then_inc(rank_rnd, 1)
                            dve.wait_ge(rank_rnd, 2 * nxt + e + 1)
                            if e == 0:
                                need(dve, out_mm, nxt * KT)
                            else:
                                dve.wait_ge(mid_mm, (nxt + 1) * KT)
                            nc.vector.scalar_tensor_tensor(out=rank_s[:], in0=rank_hi[:].bitcast(F32),
                                                           scalar=negsel[:, 0:1], in1=rank[:], op0=ALU.mult,
                                                           op1=ALU.add).then_inc(rank_done, 1)
                    for k in tile_at(XALL_AT, t):
                        if k == 0:
                            need(dve, y_tr, c * JT)
                        dve.wait_ge(xlo_done, nxt * KT + k + 1)
                        nc.vector.tensor_tensor(x1[:, np_, k], act_s[:, HI, k].bitcast(F32),
                                                act_s[:, LO, k].bitcast(F32), ALU.add).then_inc(x_all, 1)
                    for m in tile_at(MID_AT, t - 1):
                        dve.wait_ge(gel_done, nxt * KT + m + 1)
                        nc.vector.tensor_tensor(mid_s[:, LO, m], gel[:, m % 2], mid_s[:, HI, m].bitcast(F32),
                                                ALU.subtract).then_inc(mid_done, 1)
                    for m in tile_at(OUT_AT, t):
                        dve.wait_ge(out_mm, nxt * KT + m + 1)
                        dve.wait_ge(x_all, nxt * KT + m + 1)
                        nc.vector.scalar_tensor_tensor(out=x1[:, np_, m], in0=x1[:, np_, m], scalar=2.0,
                                                       in1=bulk[:, BANK_OUT[m], :], op0=ALU.mult,
                                                       op1=ALU.add).then_inc(x1_done, 1)
                    for m in tile_at(OUT_AT, t - 1):
                        dve.wait_ge(x1hi_done, nxt * KT + m + 1)
                        nc.vector.tensor_tensor(act_s[:, LO, m], x1[:, np_, m], act_s[:, HI, m].bitcast(F32),
                                                ALU.subtract).then_inc(x1lo_done, 1)

            run_chunks(dve, chunk)

        @block.tensor
        def _(pe):
            pe.wait_ge(pool_set, 3)
            pe.wait_ge(vec_in, 64)
            nc.tensor.transpose(bulk[:, 2, 0:4 * KT], vecs, ident[0:4 * KT, 0:4 * KT]).then_inc(vec_tr, 1)
            pe.wait_ge(chain, 10)
            for k in range(KT):
                nc.tensor.transpose(bulk[:, 0, k * B:(k + 1) * B], cn[:, 1, k * P:(k + 1) * P], ident[0:B, 0:B])
            for k in range(KT):
                last = nc.tensor.transpose(bulk[:, 0, (KT + k) * B:(KT + k + 1) * B], cn[:, 0, k * P:(k + 1) * P],
                                           ident[0:B, 0:B])
            last.then_inc(cond_tr, 1)
            pe.wait_ge(cT_done, 1)
            pe.wait_ge(w1_in, 16)
            for m in range(KT):
                for k in range(KT):
                    last = nc.tensor.matmul(bulk[:, 1, m * B:(m + 1) * B], w1_f[:, k, m * P:(m + 1) * P], cT[:, k, :],
                                            start=(k == 0), stop=(k == KT - 1))
            last.then_inc(hT_mm, 1)

            def turn_up(k):
                if k == 0:
                    pe.wait_ge(stage_in[1], 16)
                if k >= 2:
                    pe.wait_ge(up_split, k - 1)
                for n in range(KT):
                    last = nc.tensor.transpose(bulk[:, 4 + k % 2, n * P:(n + 1) * P],
                                               stage[:, 1, n, k * P:(k + 1) * P], ident[:])
                last.then_inc(up_tr, 1)

            def turn(n):
                pe.wait_ge(fac_done, n + 1)
                for g in range(GROUPS):
                    last = nc.tensor.transpose(turned(n)[:, g * P:(g + 1) * P],
                                               fac[:, n % 2, g].rearrange("p e b r -> p (e b r)"), ident[:])
                last.then_inc(fac_tr, 1)

            def spread(n):
                pe.wait_ge(row_done, 2 * n + 2)
                if n >= 2:
                    pe.wait_ge(fac_split, n - 1)
                wv = wrow[:, n % 2, :].rearrange("b (d r) -> b d r", r=RANK)
                for r in range(RANK):
                    last = nc.tensor.matmul(rec[:, n % 2, r * B:(r + 1) * B], wv[:, :, r], fold[:],
                                            start=True, stop=True)
                last.then_inc(fac_mm, 1)

            pe.wait_ge(fold_set, 1)
            pe.wait_ge(h_split, 1)
            for n in range(HALVES):
                for part, ready, done in ((HI, w2_hi, row_hi), (LO, w2_lo, row_mm)):
                    pe.wait_ge(ready, n + 1)
                    if part == HI and n >= 2:
                        pe.wait_ge(row_done, n - 1)
                    for k in range(KT):
                        last = nc.tensor.matmul(bulk[0:2 * B, 2 + n % 2, :], h_s[:, k].rearrange("p s b -> p (s b)"),
                                                w2_s[n % 2][:, part, k, :], start=(part == HI and k == 0),
                                                stop=(part == LO and k == KT - 1))
                    last.then_inc(done, 1)
                if n >= 3 and n % 2:
                    spread(n // 2 - 1)
                if n >= 4 and n % 2 == 0 and W2_TILES[n // 2 - 2][0] in (0, 3):
                    turn(n // 2 - 2)
                if RING <= n < RING + KT:
                    turn_up(n - RING)
            pe.wait_ge(w_split, 1)

            def rank_in(out_bank, fac_s, src, k):
                for g in range(GROUPS):
                    for p, (a, w) in enumerate(PASSES):
                        last = nc.tensor.matmul(bulk[:, out_bank, g * GC:(g + 1) * GC], fac_s[:, w, k, g, :],
                                                src[:, a, k, g * GC:(g + 1) * GC], start=(k == g == p == 0),
                                                stop=(k == KT - 1 and p == len(PASSES) - 1), skip_group_check=True)
                return last

            def dense(stage_plan, i, banks, w_s, src, rank_f, done):
                items, _, starts, ends, _ = stage_plan
                m, k, p = items[i]
                if p >= 0:
                    a, w = PASSES[p]
                    mm = nc.tensor.matmul(bulk[:, banks[m], :], w_s[:, w, k, m * P:(m + 1) * P], src[:, a, k, :],
                                          start=(i in starts), stop=(i in ends), skip_group_check=True)
                else:
                    mm = nc.tensor.matmul(bulk[:, banks[m], k * GC:(k + 1) * GC],
                                          rank_f[:, -1 - p, k, m * P:(m + 1) * P], rank_s[:, k * GC:(k + 1) * GC],
                                          start=False, stop=(i in ends), skip_group_check=True)
                if i in ends:
                    mm.then_inc(done, 1)

            def quadrant(fo, fi, first):
                for m in range(HT):
                    for k in range(fi * HT, (fi + 1) * HT):
                        n = fo * HT + m
                        if first:
                            last = nc.tensor.matmul(R[fo][:, m, 0:PARTS, :], stage[:, 1, k, n * P:(n + 1) * P],
                                                    h0s[:, k, :, :], start=(m == k == 0), stop=(k == KT - 1),
                                                    skip_group_check=True)
                            continue
                        for q in range(PARTS):
                            last = nc.tensor.matmul(R[fo][:, m, 0:PARTS, :], wh_s[:, q, k, n * P:(n + 1) * P],
                                                    hs[:, k, :, :], start=(m == k == q == 0),
                                                    stop=(k == KT - 1 and q == PARTS - 1), skip_group_check=True)
                return last

            def chunk(c, par, recur=True, bulk_on=True, y_on=True):
                nxt, np_ = c + 1, 1 - par if recur else par
                if recur and not y_on:
                    pe.wait_ge(wh_split, 1)
                for t in range(TC):
                    if recur:
                        n = c * TC + t
                        first = isinstance(n, int) and n == 0
                        need(pe, h_done, 2 * n - 1)
                        pe.wait_ge(xw_placed, 2 * n + 1)
                        quadrant(0, 0, first)
                        pe.wait_ge(xw_placed, 2 * n + 2)
                        quadrant(1, 0, first)
                        need(pe, h_done, 2 * n)
                        quadrant(0, 1, first).then_inc(rec_mm, 1)
                        quadrant(1, 1, first).then_inc(rec_mm, 1)
                    for k in tile_at(XT_SLOT, t) if bulk_on else ():
                        if k == 0:
                            need(pe, xw_done, nxt * KT - 2)
                        if k == 2:
                            need(pe, xw_done, nxt * KT)
                        for j in range(JT):
                            if k == 0:
                                pe.wait_ge(x_in[j], 16 * (nxt + 1))
                            last = nc.tensor.transpose(bulk[:, BANK_XT[k], j * P:(j + 1) * P],
                                                       xn[:, j, k * P:(k + 1) * P], ident[:])
                        last.then_inc(x_tr, 1)
                    if not recur and bulk_on:
                        if t == 0:
                            spread(LAST)
                        elif t == 1:
                            turn(LAST - 1)
                    for j in tile_at(Y_SLOT, t) if y_on else ():
                        if j == 0:
                            pe.wait_ge(sum_done, c * TC)
                            if recur:
                                pe.wait_ge(xw_done, c * KT + 3)
                        if j >= 2 and bulk_on:
                            pe.wait_ge(xlo_done, nxt * KT + j - 1)
                        for k in range(KT):
                            last = nc.tensor.transpose(bulk[:, BANK_Y[j], k * P:(k + 1) * P],
                                                       x1[:, 1 - par, k, j * P:(j + 1) * P], ident[:])
                        last.then_inc(y_tr, 1)
                    if recur and not bulk_on:
                        for k in range(IDLE_MM):
                            nc.tensor.matmul(bulk[:, BANK_XT[KT - 1], :], down_s[:, HI, 0, 0:P], act_s[:, HI, k % KT, :],
                                             start=True, stop=True)
                    if not bulk_on:
                        continue
                    for k in tile_at(U_SLOT, t):
                        if k == 0 and y_on:
                            pe.wait_ge(y_done, (c - 1) * JT + 1)
                        pe.wait_ge(xlo_done, nxt * KT + k + 1)
                        last = rank_in(BANK_U, a2_s, act_s, k)
                        if k == KT - 1:
                            last.then_inc(u_mm, 1)
                    if not recur and t == U_SLOT[-1] + 1:
                        turn(LAST)
                    if not recur and t == WH_SCALES:
                        pe.wait_ge(wmax_done, 1)
                        pe.wait_ge(fac_split, LAST + 1)
                        nc.tensor.transpose(rec[0:1, 0, 0:P], wmax[:, 2:3], ident[:]).then_inc(wmax_tr, 1)
                    if not recur and t == WH_SPREAD:
                        pe.wait_ge(sc1_done, 1)
                        nc.tensor.matmul(rec[:, 1, 0:3], ones[:], sc1[:], start=True, stop=True).then_inc(scl_mm, 1)
                    for i in MID[1].get(t, ()):
                        m, _, p = MID[0][i]
                        if i in MID[2] and m in (2, 3) and y_on:
                            pe.wait_ge(y_done, (c - 1) * JT + m)
                        if p == -1 and m == 0:
                            pe.wait_ge(rank_done, 2 * nxt + 1)
                        dense(MID, i, BANK_MID, down_s, act_s, b2_s, mid_mm)
                    for k in tile_at(V_SLOT, t):
                        if k == 0 and y_on:
                            pe.wait_ge(y_done, c * JT)
                        pe.wait_ge(mid_done, nxt * KT + k + 1)
                        last = rank_in(BANK_V, b1_s, mid_s, k)
                        if k == KT - 1:
                            last.then_inc(v_mm, 1)
                    for i in OUT[1].get(t, ()):
                        m, _, p = OUT[0][i]
                        if i == 0:
                            pe.wait_ge(rank_sel, 2 * nxt + 1)
                            if not recur:
                                pe.wait_ge(fac_split, LAST + 1)
                        if p == -1 and m == 0:
                            pe.wait_ge(rank_done, 2 * nxt + 2)
                        dense(OUT, i, BANK_OUT, up_s, mid_s, a1_s, out_mm)
                    for i in XW[1].get(t, ()):
                        m, k, p = XW[0][i]
                        if i == 0 and not recur:
                            pe.wait_ge(w_split, 2)
                        if i in XW[2] and m == 1:
                            pe.wait_ge(rank_sel, 2 * nxt + 2)
                        if p == 0 and m == 0:
                            pe.wait_ge(x1lo_done, nxt * KT + k + 1)
                        dense(XW, i, BANK_XW, wx_s, act_s, None, xw_mm)

            run_chunks(pe, chunk)


_INS = ["x", "cond_1024", "L0_cond_base_down", "L0_cond_base_up", "L0_cond_ln_gamma", "L0_cond_ln_beta", "L0_cond_W1",
        "L0_cond_bias1", "L0_cond_W2", "L0_cond_bias2", "L1_cond_Wx", "L1_cond_Wh", "L1_cond_b"]


def kernel(**inputs):
    import numpy as _np
    import concourse.bacc as _bacc
    from concourse import mybir as _mybir
    from concourse.bass_utils import run_bass_kernel_spmd as _run

    nc = _bacc.Bacc("TRN2", target_bir_lowering=False, num_devices=1)
    arrays, args = {}, []
    for name in _INS:
        a = _np.ascontiguousarray(inputs[name])
        arrays[f"in_{name}_dram"] = a
        args.append(nc.dram_tensor(f"in_{name}_dram", a.shape, _mybir.dt.from_np(a.dtype), kind="ExternalInput").ap())
    out = nc.dram_tensor("out_0_dram", inputs["x"].shape, _mybir.dt.float32, kind="ExternalOutput").ap()
    build(nc, *args, out)
    r = _run(nc, [arrays], core_ids=[0])
    return r.results[0]["out_0_dram"]
```
